# Optimizing a Trainium2 kernel written in Bass

```python
import numpy as np
import jax
import jax.numpy as jnp

def _softmax(x, axis=-1):
    return jax.nn.softmax(x, axis=axis)

def _gelu(x):
    return jax.nn.gelu(x, approximate=True)

def _silu(x):
    return jax.nn.silu(x)

def _sigmoid(x):
    return jax.nn.sigmoid(x)

def _layernorm(x, axis=-1, eps=1e-05):
    m = jnp.mean(x, axis=axis, keepdims=True)
    v = jnp.var(x, axis=axis, keepdims=True)
    return (x - m) / jnp.sqrt(v + eps)

def _scatter_add(tgt, idx, src, axis=0):
    return tgt.at[idx].add(src)

def _segment_sum(src, seg, n):
    return jax.ops.segment_sum(src, seg, n)
kernel_name = 'mk_xattn_ffn_d1_seqx_r8_167d5c'

def setup_inputs(seed: int=0):
    np.random.seed(seed)
    _w = jnp.asarray

    def _rec_inputs():
        import jax
        import jax.numpy as jnp
        _rk = jax.random.key(seed)
        x = 7.22e-05 + 1 * jax.random.normal(jax.random.fold_in(_rk, 1), (32, 128, 128), jnp.float32)
        _lenS = 128 - jax.random.randint(jax.random.fold_in(_rk, 7), (32,), 0, max(1, 128 // 4) + 1, jnp.int32)
        _lenS2 = 128 - jax.random.randint(jax.random.fold_in(_rk, 8), (32,), 0, max(1, 128 // 4) + 1, jnp.int32)
        _ctx_1024P = jax.random.normal(jax.random.fold_in(_rk, 11), (32, 16, 128), jnp.float32)
        _ctx_1024c = jax.random.dirichlet(jax.random.fold_in(_rk, 511), 0.3 * jnp.ones((16,), jnp.float32), (32, 128))
        _ctx_1024t = jnp.einsum('bsk,bkd->bsd', _ctx_1024c, _ctx_1024P)
        _ctx_1024t = _ctx_1024t * jax.lax.rsqrt(jnp.mean(jnp.square(_ctx_1024t)) + 1e-12) * 0.953939
        ctx_1024 = 4.13588e-05 + 0.999923 * (_ctx_1024t + 0.3 * jax.random.normal(jax.random.fold_in(_rk, 611), (32, 128, 128), jnp.float32))
        return (x, ctx_1024)
    x, ctx_1024 = _rec_inputs()

    def _L0_xattn_setup():
        import jax, jax.numpy as jnp
        import numpy as np
        HIDDEN = 128
        HEADS = 16
        HEAD_DIM = HIDDEN // HEADS
        key = jax.random.key(seed)
        ks = jax.random.split(key, 12)
        B, S, D = (4, 256, HIDDEN)
        scale = 1.0 / np.sqrt(D)
        inp = {'q': jax.random.normal(ks[0], (B, S, D), jnp.float32), 'k': jax.random.normal(ks[1], (B, S, D), jnp.float32), 'v': jax.random.normal(ks[2], (B, S, D), jnp.float32), 'Wq': jax.random.normal(ks[3], (D, D), jnp.float32) * scale, 'bq': jnp.zeros((D,), jnp.float32), 'Wk': jax.random.normal(ks[4], (D, D), jnp.float32) * scale, 'bk': jnp.zeros((D,), jnp.float32), 'Wv': jax.random.normal(ks[5], (D, D), jnp.float32) * scale, 'bv': jnp.zeros((D,), jnp.float32), 'Wo': jax.random.normal(ks[6], (D, D), jnp.float32) * scale, 'bo': jnp.zeros((D,), jnp.float32)}
        return inp
    _L0_xattn_all = _L0_xattn_setup()
    _L0_xattn_in = {k: v for k, v in _L0_xattn_all.items() if k in ('Wq', 'bq', 'Wk', 'bk', 'Wv', 'bv', 'Wo', 'bo')}
    del _L0_xattn_all

    def _L0_ffn_setup():
        import jax, jax.numpy as jnp
        import numpy as np
        TOP_K = 2
        CAP_FACTOR = 1.25
        MIN_CAPACITY = 4
        key = jax.random.key(seed)
        k1, k2, k3, k4 = jax.random.split(key, 4)
        B, T, C, E = (8, 256, 128, 8)
        x = jax.random.normal(k1, (B, T, C), dtype=jnp.float32)
        w_g = jax.random.normal(k2, (E, C), dtype=jnp.float32) * 0.02
        c_fc = jax.random.normal(k3, (E, C, 4 * C), dtype=jnp.float32) * 0.02
        c_proj = jax.random.normal(k4, (E, 4 * C, C), dtype=jnp.float32) * 0.02
        return {'x': x, 'w_g': w_g, 'c_fc': c_fc, 'c_proj': c_proj}
    _L0_ffn_all = _L0_ffn_setup()
    _L0_ffn_in = {k: v for k, v in _L0_ffn_all.items() if k in ('w_g', 'c_fc', 'c_proj')}
    del _L0_ffn_all
    return {'x': x, 'ctx_1024': ctx_1024, 'L0_xattn_Wq': _L0_xattn_in['Wq'], 'L0_xattn_bq': _L0_xattn_in['bq'], 'L0_xattn_Wk': _L0_xattn_in['Wk'], 'L0_xattn_bk': _L0_xattn_in['bk'], 'L0_xattn_Wv': _L0_xattn_in['Wv'], 'L0_xattn_bv': _L0_xattn_in['bv'], 'L0_xattn_Wo': _L0_xattn_in['Wo'], 'L0_xattn_bo': _L0_xattn_in['bo'], 'L0_ffn_w_g': _L0_ffn_in['w_g'], 'L0_ffn_c_fc': _L0_ffn_in['c_fc'], 'L0_ffn_c_proj': _L0_ffn_in['c_proj']}

def reference(x, ctx_1024, L0_xattn_Wq, L0_xattn_bq, L0_xattn_Wk, L0_xattn_bk, L0_xattn_Wv, L0_xattn_bv, L0_xattn_Wo, L0_xattn_bo, L0_ffn_w_g, L0_ffn_c_fc, L0_ffn_c_proj):
    import jax
    import jax.numpy as jnp

    def _L0_xattn_ref(q, k, v, Wq, bq, Wk, bk, Wv, bv, Wo, bo):
        import jax, jax.numpy as jnp
        import numpy as np
        HIDDEN = 128
        HEADS = 16
        HEAD_DIM = HIDDEN // HEADS
        B, S, D = q.shape
        H, Dh = (HEADS, HEAD_DIM)
        Q = q @ Wq + bq
        K = k @ Wk + bk
        V = v @ Wv + bv
        Qh = Q.reshape(B, S, H, Dh).transpose(0, 2, 1, 3)
        Kh = K.reshape(B, S, H, Dh).transpose(0, 2, 1, 3)
        Vh = V.reshape(B, S, H, Dh).transpose(0, 2, 1, 3)
        scores = jnp.einsum('bhqd,bhkd->bhqk', Qh, Kh) / jnp.sqrt(jnp.float32(Dh))
        attn = jax.nn.softmax(scores, axis=-1)
        ctx = jnp.einsum('bhqk,bhkd->bhqd', attn, Vh)
        out = ctx.transpose(0, 2, 1, 3).reshape(B, S, D)
        return out @ Wo + bo

    def _L0_ffn_ref(x, w_g, c_fc, c_proj):
        import jax, jax.numpy as jnp
        import numpy as np
        TOP_K = 2
        CAP_FACTOR = 1.25
        MIN_CAPACITY = 4
        B, T, C = x.shape
        E = w_g.shape[0]
        N = B * T
        capacity = max(MIN_CAPACITY, int(CAP_FACTOR * N * TOP_K / E))
        xf = x.reshape(N, C)
        logits = xf @ w_g.T
        top_logits, top_idx = jax.lax.top_k(logits, TOP_K)
        router_probs = jax.nn.softmax(top_logits, axis=-1)
        oh = jax.nn.one_hot(top_idx, E, dtype=jnp.int32)
        oh_t = oh.transpose(1, 0, 2).reshape(TOP_K * N, E)
        pos = jnp.cumsum(oh_t, axis=0).reshape(TOP_K, N, E).transpose(1, 0, 2)
        rank = jnp.sum((pos - 1) * oh, axis=-1)
        valid = rank < capacity
        probs_masked = router_probs * valid.astype(router_probs.dtype)
        rank_c = jnp.clip(rank, 0, capacity - 1)
        contrib = xf[:, None, :] * valid[..., None].astype(xf.dtype)
        buf = jnp.zeros((E, capacity, C), dtype=xf.dtype).at[top_idx, rank_c].add(contrib)
        h = jnp.einsum('ecd,edf->ecf', buf, c_fc)
        h = jnp.square(jax.nn.relu(h))
        expert_out = jnp.einsum('ecf,efd->ecd', h, c_proj)
        gathered = expert_out[top_idx, rank_c]
        out = jnp.sum(gathered * probs_masked[..., None], axis=1)
        return out.reshape(B, T, C)
    x = x + _L0_xattn_ref(_layernorm(x, axis=-1), ctx_1024, ctx_1024, L0_xattn_Wq, L0_xattn_bq, L0_xattn_Wk, L0_xattn_bk, L0_xattn_Wv, L0_xattn_bv, L0_xattn_Wo, L0_xattn_bo)
    x = x + _L0_ffn_ref(_layernorm(x, axis=-1), L0_ffn_w_g, L0_ffn_c_fc, L0_ffn_c_proj)
    return x

_drawn_inputs = setup_inputs


def setup_inputs(seed=0):
    import zlib

    import numpy as np

    out = dict(_drawn_inputs(seed))
    spreads = {'L0_xattn_bq': (0.0, 0.346),
     'L0_xattn_bk': (0.0, 0.8),
     'L0_xattn_bv': (0.0, 0.1),
     'L0_xattn_bo': (0.0, 0.1)}
    factors = {'L0_ffn_w_g': 3.722, 'L0_ffn_c_fc': 3.583, 'L0_ffn_c_proj': 3.301}
    for name, (base, spread) in spreads.items():
        noise = np.random.default_rng([zlib.crc32(name.encode()), seed]).standard_normal(out[name].shape)
        drawn = base * np.exp(spread * noise) if base else spread * noise
        out[name] = jnp.asarray(drawn.astype(out[name].dtype))
    for name, factor in factors.items():
        out[name] = (out[name] * factor).astype(out[name].dtype)
    return out
```

```python
from contextlib import ExitStack

import concourse.bass as bass
from concourse import mybir

ALU = mybir.AluOpType
ACT = mybir.ActivationFunctionType
AX = mybir.AxisListType
F32 = mybir.dt.float32
BF16 = mybir.dt.bfloat16
I32 = mybir.dt.int32
U32 = mybir.dt.uint32

P = 128
Q_TERMS = (0, 1, 2, 0, 1, 0)
K_TERMS = (0, 0, 0, 1, 1, 2)
EPS = 1e-5
TOP_K = 2


class At:

    def __init__(self, base, regs=None):
        self.base, self.regs = base, regs

    def _of(self, k, const):
        return const if self.regs is None else self.regs[k] + const

    def times(self, k, plus=0):
        return self._of(4 * k, k * self.base + plus)

    def rounds16(self, plus=0):
        return self._of(16, 16 * (self.base // 4 + 1) + plus)

    def __add__(self, n):
        return At(self.base + n, self.regs)

    @property
    def known(self):
        return self.regs is None


def xattn_moe_kernel(nc, x, ctx, Wq, bq, Wk, bk, Wv, bv, Wo, bo, w_g, c_fc, c_proj, out):
    B, S, D = x.shape
    E, _, F = c_fc.shape
    H = 16
    DH = D // H
    NF = F // P
    N = B * S
    CAP = int(1.25 * N * TOP_K / E)
    G = 4
    NG = B // G
    NT = len(Q_TERMS)
    KR = NT * DH
    KC = 96
    HC = 4
    NC = H // HC
    VW = 32
    RW = 132
    CH = 256
    NCH = CAP // CH
    SCALE = 1.0 / float(DH) ** 0.5
    FAR = 100000
    assert S == P and D == P and E == 8 and CAP % CH == 0 and B % 4 == 0

    def dram(name, shape, dt):
        return nc.dram_tensor(name, shape, dt, kind="Internal").ap()

    q_stack_d = dram("q_stack_d", (B, NT, P, S), BF16)
    k_stack_d = dram("k_stack_d", (B, NT, P, S), BF16)
    negmax_d = dram("negmax_d", (B, 3, H * S), BF16)
    slots_d = dram("slots_d", (E * CAP, RW), F32)
    result_d = dram("result_d", (TOP_K * N, D), F32)

    with ExitStack() as es:
        def sb(name, shape, dt=F32):
            return es.enter_context(nc.sbuf_tensor(name, shape, dt))

        def sem(name):
            return es.enter_context(nc.semaphore(name))

        bank = [es.enter_context(nc.psum_tensor(f"bank{i}", [P, 512], F32)) for i in range(8)]

        ident = sb("ident", [P, P])
        identb = sb("identb", [P, P], BF16)
        before = sb("before", [P, P], BF16)
        onesb = sb("onesb", [P, P], BF16)
        ones_rows = sb("ones_rows", [3, H * S], BF16)
        ioE = sb("ioE", [P, E])
        seg = sb("seg", [P, E, TOP_K * B])
        ids = sb("ids", [P, TOP_K, B], I32)
        mhalf = sb("mhalf", [P, G])
        wq_raw = sb("wq_raw", [P, D])
        wk_raw = sb("wk_raw", [P, D])
        wq_s = sb("wq_s", [P, D])
        wk_s = sb("wk_s", [P, D])
        wv_s = sb("wv_s", [P, D])
        wo_s = sb("wo_s", [P, D])
        bqk_raw = sb("bqk_raw", [1, 2, D])
        bqk_row = sb("bqk_row", [1, 2, D])
        bq_col = sb("bq_col", [P, 1])
        bk_col = sb("bk_col", [P, 1])
        bv_all = sb("bv_all", [P, D])
        bo_all = sb("bo_all", [P, D])
        wg_raw = sb("wg_raw", [E, D])
        wgT = sb("wgT", [P, E])
        empty = sb("empty", [P, 4, RW])
        zeros = sb("zeros", [P, 4, D])

        xr = sb("xr", [P, B, D])
        c_in = sb("c_in", [P, G, D])
        v_all = sb("v_all", [P, B, D])
        stA = sb("stA", [P, G, 6])
        mvA = sb("mvA", [P, G, 2])
        vareA = sb("vareA", [P, G])
        rstdA = sb("rstdA", [P, G])
        xnA = sb("xnA", [P, G, D])
        xTA = sb("xTA", [P, G * S])
        cTA = sb("cTA", [P, G * S])
        qf = sb("qf", [P, G * S])
        kf = sb("kf", [P, G * S])
        qr = sb("qr", [P, G * S])
        kr = sb("kr", [P, G * S])
        qp = sb("qp", [P, 3, G * S], BF16)
        kp = sb("kp", [P, 3, G * S], BF16)

        qs = [sb(f"qs{i}", [KC, H * S], BF16) for i in range(4)]
        ks = [sb(f"ks{i}", [KC, H * S], BF16) for i in range(4)]
        km = [sb(f"km{i}", [KC, H * S], BF16) for i in range(4)]
        va = [sb(f"va{i}", [P, H, VW]) for i in range(2)]
        mxt = sb("mxt", [P, H])
        nrem = sb("nrem", [P, H])
        nparts_pad = sb("nparts_pad", [P, P], BF16)
        nparts = nparts_pad[:, 0:3 * H].rearrange("p (t h) -> p t h", t=3)
        nT = [sb(f"nT{i}", [3 * H, S], BF16) for i in range(4)]
        pr = [sb(f"pr{i}", [P, HC * S]) for i in range(4)]
        avs = sb("avs", [P, NC * S])
        rden = sb("rden", [P, H])
        cn = sb("cn", [P, D])
        cnT = sb("cnT", [P, S])
        x1 = [sb(f"x1_{i}", [P, D]) for i in range(2)]
        st = sb("st", [P, 6])
        mv = sb("mv", [P, 2])
        vare = sb("vare", [P, 1])
        rstd = sb("rstd", [P, 1])
        xs = [sb(f"xs{i}", [P, D]) for i in range(2)]
        xsT = sb("xsT", [P, S])
        top8 = sb("top8", [P, E])
        idx8 = sb("idx8", [P, E], U32)
        rows = [sb(f"rows{k}", [P, B, RW]) for k in range(TOP_K)]

        tv = sb("tv", [P, TOP_K, B])
        ti = sb("ti", [P, TOP_K, B])
        oh = sb("oh", [P, TOP_K * B, E], BF16)
        cnt = sb("cnt", [P, E, TOP_K * B])
        cum = sb("cum", [P, E, TOP_K * B])
        rk = sb("rk", [P, TOP_K * B, E])
        rank = sb("rank", [P, TOP_K * B])
        valid = sb("valid", [P, TOP_K, B])
        slot = sb("slot", [P, TOP_K * B])
        sloti = sb("sloti", [P, TOP_K * B], I32)
        pdiff = sb("pdiff", [P, B])
        pe2 = sb("pe2", [P, B])
        psumr = sb("psumr", [P, B])
        prob = sb("prob", [P, TOP_K, B])

        w1 = [sb(f"w1_{i}", [P, F]) for i in range(2)]
        w2 = [sb(f"w2_{i}", [P, NF, D]) for i in range(2)]
        br = [sb(f"br{i}", [P, 2, RW]) for i in range(2)]
        dst = [sb(f"dst{i}", [P, 2], I32) for i in range(2)]
        bT = [sb(f"bT{i}", [P, CH]) for i in range(2)]
        room = v_all[:].rearrange("p b d -> p (b d)").rearrange("p (i f c) -> p i f c", i=4, f=NF)
        hr = [room[:, i] for i in range(2)]
        hs = [room[:, 2 + i] for i in range(2)]
        ys = [sb(f"ys{i}", [P, 2, D]) for i in range(2)]

        ya = [[xTA, cTA], [qf, kf]]
        ya = [[t[:].rearrange("p (g d) -> p g d", g=G) for t in pair] for pair in ya]

        names = """w_in b_in g_in c_ready e_ready wperm bcol bcol_ps wgT_ps fills
            x_in c_inn stA_done mvA_done vareA_done rstdA_done xnA_done xbo
            xT_ps cT_ps xT_out cT_out q_ps k_ps v_ps qf_done kf_done q1 k1 qr_done kr_done q2 k2 q3 k3
            v_out q_put k_put
            s1 mx n1 nr n2 n3 nT_ps nT_out s2 ex av va_in av_out nat rec cn_done cnT_ps cnT_out wo_ps x1_done
            st_done mv_done vare_done rstd_done xs_done x1_kept xs_kept xsT_ps xsT_out lg top_done idx_done
            top_kept
            rt rk_ps cnt_ps pe_done rows1 sc_done
            br_in0 br_in1 w_in0 w_in1 bT_ps bT_out h_ps hr_done hs_done y_ps y_out dst_done put0 put1
            ya_in0 ya_in1 e1 e2 out_put0 out_put1 settled""".split()
        s = {n: sem(n) for n in names}
        q_in = [sem(f"q_in{i}") for i in range(4)]
        k_in = [sem(f"k_in{i}") for i in range(4)]
        km_in = [sem(f"km_in{i}") for i in range(4)]
        m_put = [sem(f"m_put{i}") for i in range(4)]
        m_in = [sem(f"m_in{i}") for i in range(4)]

        def need(eng, what, value):
            if not isinstance(value, int) or value > 0:
                eng.wait_ge(what, value)

        def settle(eng):
            eng.sem_inc(s["settled"], 1)

        def groups(eng, body):
            body(At(0))
            with eng.Fori(1, NG) as g:
                r = eng.snap(g * 4)
                r4 = eng.snap(g * 16)
                body(At(0, {4: g, 16: r, 64: r4}))

        def steps(eng, body, first, last, lo=2, hi=29):
            for j in range(first, lo):
                body(At(j))
            with eng.Fori(0, (hi + 1 - lo) // 4) as r:
                regs = {4: eng.snap(r * 4), 16: eng.snap(r * 16)}
                for u in range(4):
                    body(At(lo + u, regs))
            for j in range(hi + 1, last + 1):
                body(At(j))

        def pairs(eng, body):
            body(lambda k, plus: plus)
            with eng.Fori(1, E // 2) as pair:
                held = {}

                def of(k, plus):
                    if k not in held:
                        held[k] = eng.snap(pair * k)
                    return held[k] + plus

                for k in (2 * NCH, 16 * NCH, 32 * NCH, 4 * NCH, 32, 2):
                    of(k, 0)
                body(of)

        def live(b):
            return not b.known or 0 <= b.base < B

        def next_expert(eng, of, plus):
            e = of(2, plus)
            return e % E if isinstance(e, int) else eng.snap(e % E)

        def _times96(eng, g):
            return 16 * NT * g.base if g.known else eng.snap(g.regs[4] * (16 * NT))

        def _twice(eng, b):
            return 2 * b.base if b.known else b.times(1) * 2

        block = es.enter_context(nc.Block())

        @block.sync
        def _(sp):
            for w, d in ((wq_raw, Wq), (wk_raw, Wk), (wv_s, Wv), (wo_s, Wo)):
                sp.dma_start(w[:], d).then_inc(s["w_in"], 16)
            sp.dma_start(bqk_raw[:, 0, :], bq.unsqueeze(0)).then_inc(s["b_in"], 16)
            sp.dma_start(bqk_raw[:, 1, :], bk.unsqueeze(0)).then_inc(s["b_in"], 16)
            sp.dma_start(bv_all[:], bv.partition_broadcast(P)).then_inc(s["b_in"], 16)
            sp.dma_start(bo_all[:], bo.partition_broadcast(P)).then_inc(s["b_in"], 16)
            sp.dma_start(wg_raw[:], w_g).then_inc(s["g_in"], 16)

            xg = x.rearrange("b s d -> s b d")
            cg = ctx.rearrange("b s d -> s b d")

            def load(g):
                need(sp, s["cT_ps"], g.times(1))
                b0 = g.times(4)
                sp.dma_start(xr[:, bass.ds(b0, G), :], xg[:, bass.ds(b0, G), :]).then_inc(s["x_in"], 16)
                sp.dma_start(c_in[:], cg[:, bass.ds(b0, G), :]).then_inc(s["c_inn"], 16)

            def store(g):
                b0 = g.times(4)
                for done, parts, terms, stack, put in ((("q1", "q2", "q3"), qp, Q_TERMS, q_stack_d, "q_put"),
                                                       (("k1", "k2", "k3"), kp, K_TERMS, k_stack_d, "k_put")):
                    for part in done:
                        need(sp, s[part], g.times(1, 1))
                    for t, part in enumerate(terms):
                        sp.dma_start(stack[bass.ds(b0, G), t, :, :].rearrange("b r q -> r b q"),
                                     parts[:, part, :].rearrange("p (b q) -> p b q", b=G)
                                     ).then_inc(s[put], 16)

            load(At(0))
            with sp.Fori(1, NG) as g:
                r4, r16 = sp.snap(g * 4), sp.snap(g * 16)
                now = At(0, {4: g, 16: r4, 64: r16})
                load(now)
                store(now + (-1))
            store(At(NG - 1))

            sp.wait_ge(s["e_ready"], 1)
            sp.dma_start(slots_d.rearrange("(p a b) w -> p a (b w)", p=P, b=4),
                         empty[:].rearrange("p b w -> p (b w)").unsqueeze(1)
                         .to_broadcast([P, E * CAP // P // 4, 4 * RW])).then_inc(s["fills"], 16)
            sp.dma_start(result_d.rearrange("(p a b) w -> p a (b w)", p=P, b=4),
                         zeros[:].rearrange("p b w -> p (b w)").unsqueeze(1)
                         .to_broadcast([P, TOP_K * N // P // 4, 4 * D])).then_inc(s["fills"], 16)

            sp.wait_ge(s["q_put"], 16 * NT * NG)
            sp.wait_ge(s["k_put"], 16 * NT * NG)
            sp.wait_ge(s["c_ready"], 1)
            for i in range(4):
                sp.dma_start(ks[i][KR:KR + 3, :], ones_rows[:]).then_inc(k_in[i], 16)

            def load_stacks(b):
                i = b.base % 4
                if not live(b):
                    return
                need(sp, s["s2"], b.times(4, -12))
                row = bass.ds(b.times(1), 1)
                for t, src, got in ((qs, q_stack_d, q_in), (km, k_stack_d, km_in), (ks, k_stack_d, k_in)):
                    sp.dma_start(t[i][0:KR, :], src[row].rearrange("o t (d h) q -> (o t d) (h q)", d=DH)
                                 ).then_inc(got[i], 16)

            def max_rows(b):
                if not live(b):
                    return
                i = b.base % 4
                row = bass.ds(b.times(1), 1)
                sp.wait_ge(s["nT_out"], b.times(1, 1))
                sp.dma_start(negmax_d[row].rearrange("o t (h q) -> (o t h) q", h=H), nT[i][:]
                             ).then_inc(m_put[i], 16)
                sp.wait_ge(m_put[i], b.rounds16())
                sp.dma_start(qs[i][KR:KR + 3, :], negmax_d[row].rearrange("o t r -> (o t) r")
                             ).then_inc(m_in[i], 16)

            for b in range(2):
                load_stacks(At(b))

            def step(j):
                max_rows(j + 1)
                load_stacks(j + 3)

            steps(sp, step, -1, 31, 1, 28)

            def load_weights(e, i):
                sp.dma_start(w1[i][:], c_fc[bass.ds(e, 1)].rearrange("o c f -> (o c) f")).then_inc(s[f"w_in{i}"], 16)
                sp.dma_start(w2[i][:], c_proj[bass.ds(e, 1)].rearrange("o (n f) c -> (o f) n c", n=NF)
                             ).then_inc(s[f"w_in{i}"], 16)

            load_weights(0, 0)
            load_weights(1, 1)
            sp.wait_ge(s["sc_done"], 16 * TOP_K * B)
            slot_rows = slots_d.rearrange("(n t p) w -> n p t w", t=2, p=P)

            def chunks(of):
                for u in range(2 * NCH):
                    need(sp, s["bT_ps"], of(2 * NCH, u - 1))
                    need(sp, s["dst_done"], of(2 * NCH, u - 1))
                    sp.dma_start(br[u % 2][:], slot_rows[bass.ds(of(2 * NCH, u), 1)].rearrange("o p t w -> (o p) t w")
                                 ).then_inc(s[f"br_in{u % 2}"], 16)
                    if u == NCH + 1:
                        sp.wait_ge(s["y_ps"], of(2 * NCH, NCH))
                        load_weights(next_expert(sp, of, 2), 0)
                sp.wait_ge(s["y_ps"], of(2 * NCH, 2 * NCH))
                load_weights(next_expert(sp, of, 3), 1)

            pairs(sp, chunks)
            sp.wait_ge(s["w_in0"], 32 * (E // 2 + 1))
            sp.wait_ge(s["w_in1"], 32 * (E // 2 + 1))

            sp.wait_ge(s["put0"], 32 * (E * NCH // 2))
            sp.wait_ge(s["put1"], 32 * (E * NCH // 2))
            res = result_d.rearrange("(k g t p) d -> k g p t d", k=TOP_K, t=G, p=P)
            outg = out.rearrange("(g t) s d -> g s t d", t=G)
            for g in range(NG + 1):
                if g < NG:
                    need(sp, s["e2"], G * (g - 1))
                    for k in range(TOP_K):
                        sp.dma_start(ya[g % 2][k], res[k, g]).then_inc(s[f"ya_in{g % 2}"], 16)
                if g >= 1:
                    sp.wait_ge(s["e2"], G * g)
                    sp.dma_start(outg[g - 1], xr[:, G * (g - 1):G * g, :]).then_inc(s[f"out_put{g % 2}"], 16)
            sp.wait_ge(s["out_put0"], 16 * NG // 2)
            sp.wait_ge(s["out_put1"], 16 * NG // 2)

        @block.gpsimd
        def _(pool):
            pool.memset(ident[:], 0.0).then_inc(s["rt"], 1)
            pool.memset(before[:], 1.0).then_inc(s["rt"], 1)
            pool.memset(seg[:], 1.0).then_inc(s["rt"], 1)
            pool.memset(onesb[:], 1.0).then_inc(s["rt"], 1)
            pool.memset(ones_rows[:], 1.0).then_inc(s["rt"], 1)
            pool.memset(mhalf[:], -0.5).then_inc(s["rt"], 1)
            pool.memset(zeros[:], 0.0).then_inc(s["rt"], 1)
            pool.memset(empty[:], 0.0).then_inc(s["rt"], 1)
            pool.iota(ids[:], [[N, TOP_K], [P, B]], base=0, channel_multiplier=1).then_inc(s["rt"], 1)
            pool.iota(ioE[:], [[1, E]], base=0, channel_multiplier=0,
                      allow_small_or_imprecise_dtypes=True).then_inc(s["rt"], 1)
            for i in range(4):
                for t in (qs, ks, km):
                    pool.memset(t[i][:], 0.0).then_inc(s["rt"], 1)
            for i in range(2):
                pool.memset(va[i][:], 0.0).then_inc(s["rt"], 1)
            pool.memset(nparts_pad[:], 0.0).then_inc(s["rt"], 1)
            pool.wait_ge(s["rt"], 25)
            pool.affine_select(out=ident[:], in_=ident[:], compare_op=ALU.not_equal, fill=1.0, base=0,
                               pattern=[[-1, P]], channel_multiplier=1).then_inc(s["rt"], 1)
            pool.affine_select(out=before[:], in_=before[:], compare_op=ALU.is_gt, fill=0.0, base=0,
                               pattern=[[1, P]], channel_multiplier=-1).then_inc(s["rt"], 1)
            pool.memset(seg[:, :, 0:1], 0.0).then_inc(s["rt"], 1)
            for i in range(2):
                pool.memset(va[i][:, :, DH:DH + 1], 1.0).then_inc(s["rt"], 1)
            pool.iota(empty[:, :, D:D + 1].bitcast(I32), [[0, 4], [0, 1]], base=TOP_K * N + FAR % 8192,
                      channel_multiplier=0).then_inc(s["rt"], 1)
            pool.wait_ge(s["rt"], 31)
            pool.tensor_copy(identb[:], ident[:]).then_inc(s["rt"], 1)
            pool.wait_ge(s["rt"], 32)
            pool.sem_inc(s["c_ready"], 1)
            pool.sem_inc(s["e_ready"], 1)

            pool.wait_ge(s["w_in"], 64)
            pool.wait_ge(s["b_in"], 64)
            for w, r in ((wq_s, wq_raw), (wk_s, wk_raw)):
                pool.tensor_copy(w[:].rearrange("p (d h) -> p d h", d=DH),
                                 r[:].rearrange("p (h d) -> p d h", d=DH)).then_inc(s["wperm"], 1)
            for i in range(2):
                pool.tensor_copy(bqk_row[:, i, :].rearrange("p (d h) -> p d h", d=DH),
                                 bqk_raw[:, i, :].rearrange("p (h d) -> p d h", d=DH)).then_inc(s["wperm"], 1)

            def stage_a(g):
                pool.wait_ge(s["mvA_done"], g.times(4, G))
                settle(pool)
                pool.tensor_scalar(vareA[:], mvA[:, :, 1], EPS, None, ALU.add).then_inc(s["vareA_done"], 1)
                pool.wait_ge(s["vareA_done"], g.times(1, 1))
                need(pool, s["xnA_done"], g.times(4))
                pool.tensor_tensor(rstdA[:], vareA[:], mhalf[:], ALU.pow).then_inc(s["rstdA_done"], 1)
                pool.wait_ge(s["xnA_done"], g.times(4, G))
                xg = xr[:, bass.ds(g.times(4), G), :]
                pool.tensor_tensor(xg, xg, bo_all[:].unsqueeze(1).to_broadcast([P, G, D]), ALU.add
                                   ).then_inc(s["xbo"], 1)
                pool.wait_ge(s["k2"], g.times(1, 1))
                need(pool, s["k_put"], _times96(pool, g))
                pool.tensor_tensor(kp[:, 2, :], kr[:], kp[:, 1, :], ALU.subtract).then_inc(s["k3"], 1)

            groups(pool, stage_a)

            def step(j):
                b = j + 1
                if live(b):
                    pool.wait_ge(s["v_out"], NG)
                    need(pool, s["av"], b.times(4, -4))
                    if b.known and b.base < 2:
                        pool.wait_ge(s["rt"], 31)
                    pool.tensor_copy(va[b.base % 2][:, :, 0:DH],
                                     v_all[:, bass.ds(b.times(1), 1), :].rearrange("p o (h d) -> p (o h) d", d=DH)
                                     ).then_inc(s["va_in"], 1)
                b = j + (-2)
                if live(b):
                    pool.wait_ge(s["idx_done"], b.times(1, 1))
                    col = bass.ds(b.times(1), 1)
                    pool.tensor_copy(tv[:, :, col], top8[:, 0:TOP_K].unsqueeze(2)).then_inc(s["top_kept"], 1)
                    pool.tensor_copy(ti[:, :, col], idx8[:, 0:TOP_K].unsqueeze(2)).then_inc(s["top_kept"], 1)
                b = j + (-1)
                if live(b):
                    pool.wait_ge(s["mv_done"], b.times(1, 1))
                    settle(pool)
                    pool.tensor_scalar(vare[:], mv[:, 1:2], EPS, None, ALU.add).then_inc(s["vare_done"], 1)
                    pool.wait_ge(s["vare_done"], b.times(1, 1))
                    need(pool, s["xs_done"], b.times(1))
                    pool.tensor_tensor(rstd[:], vare[:], mhalf[:, 0:1], ALU.pow).then_inc(s["rstd_done"], 1)
                    row = bass.ds(b.times(1), 1)
                    pool.tensor_copy(xr[:, row, :], x1[b.base % 2][:].unsqueeze(1)).then_inc(s["x1_kept"], 1)
                    pool.wait_ge(s["xs_done"], b.times(1, 1))
                    pool.tensor_copy(rows[0][:, row, 0:D], xs[b.base % 2][:].unsqueeze(1)).then_inc(s["xs_kept"], 1)

            steps(pool, step, -1, 33)

            pool.wait_ge(s["rows1"], 5)
            pool.wait_ge(s["fills"], 32)
            for k in range(TOP_K):
                for b in range(B):
                    col = k * B + b
                    pool.indirect_dma_start(slots_d, bass.IndirectOffsetOnAxis(ap=sloti[:, col:col + 1], axis=0),
                                            rows[k][:, b, :], None, bounds_check=E * CAP - 1, oob_is_err=False
                                            ).then_inc(s["sc_done"], 16)

            def scatters(of):
                for u in range(2 * NCH):
                    pool.wait_ge(s["y_out"], of(2 * NCH, u + 1))
                    settle(pool)
                    for t in range(2):
                        pool.indirect_dma_start(result_d,
                                                bass.IndirectOffsetOnAxis(ap=dst[u % 2][:, t:t + 1], axis=0),
                                                ys[u % 2][:, t, :], None, bounds_check=TOP_K * N - 1,
                                                oob_is_err=False).then_inc(s[f"put{u % 2}"], 16)

            pairs(pool, scatters)

        @block.scalar
        def _(act):
            act.wait_ge(s["bcol_ps"], 2)
            act.wait_ge(s["wgT_ps"], 1)
            act.copy(bq_col[:], bank[7][:, 0:1]).then_inc(s["bcol"], 1)
            act.copy(bk_col[:], bank[7][:, 1:2]).then_inc(s["bcol"], 1)
            act.copy(wgT[:], bank[7][:, 8:8 + E]).then_inc(s["bcol"], 1)
            act.wait_ge(s["bcol"], 3)

            def stage_a(g):
                act.wait_ge(s["xT_ps"], g.times(1, 1))
                need(act, s["q_ps"], g.times(1))
                act.copy(xTA[:], bank[0][:]).then_inc(s["xT_out"], 1)
                act.wait_ge(s["q_ps"], g.times(1, 1))
                put = _times96(act, g)
                need(act, s["q3"], g.times(1))
                act.activation(qf[:], bank[2][:], ACT.Identity, bias=bq_col[:]).then_inc(s["qf_done"], 1)
                need(act, s["q_put"], put)
                act.activation(qp[:, 0, :], bank[2][:], ACT.Identity, bias=bq_col[:]).then_inc(s["q1"], 1)
                act.wait_ge(s["k_ps"], g.times(1, 1))
                need(act, s["k3"], g.times(1))
                act.activation(kf[:], bank[3][:], ACT.Identity, bias=bk_col[:]).then_inc(s["kf_done"], 1)
                need(act, s["k_put"], put)
                act.activation(kp[:, 0, :], bank[3][:], ACT.Identity, bias=bk_col[:]).then_inc(s["k1"], 1)
                act.wait_ge(s["qr_done"], g.times(1, 1))
                act.copy(qp[:, 1, :], qr[:]).then_inc(s["q2"], 1)
                act.wait_ge(s["kr_done"], g.times(1, 1))
                act.copy(kp[:, 1, :], kr[:]).then_inc(s["k2"], 1)

            groups(act, stage_a)

            def exps(b, c):
                act.wait_ge(s["s2"], b.times(4, c + 1))
                need(act, s["av"], b.times(4, c - 3))
                act.activation(pr[c][:], bank[2 + c % 2][:], ACT.Exp, scale=SCALE).then_inc(s["ex"], 1)

            def step(j):
                b = j + 1
                if live(b):
                    act.wait_ge(s["nT_ps"], b.times(1, 1))
                    i = b.base % 4
                    need(act, m_put[i], b.rounds16(-16))
                    act.copy(nT[i][:], bank[7][0:3 * H, 0:S // 2].bitcast(BF16)).then_inc(s["nT_out"], 1)
                if live(j):
                    exps(j, 0)
                b = j + (-2)
                if live(b):
                    act.wait_ge(s["xsT_ps"], b.times(1, 1))
                    need(act, s["lg"], b.times(1))
                    act.copy(xsT[:], bank[7][:, 128:256]).then_inc(s["xsT_out"], 1)
                if live(j):
                    exps(j, 1)
                b = j + (-1)
                if live(b):
                    act.wait_ge(s["cnT_ps"], b.times(1, 1))
                    need(act, s["wo_ps"], b.times(1))
                    act.copy(cnT[:], bank[6][:, 0:128]).then_inc(s["cnT_out"], 1)
                if live(j):
                    exps(j, 2)
                    exps(j, 3)
                    act.wait_ge(s["av"], j.times(4, 4))
                    need(act, s["nat"], j.times(1))
                    act.copy(avs[:], bank[4][:]).then_inc(s["av_out"], 1)

            steps(act, step, -1, 33)

            act.wait_ge(s["rt"], 33)
            act.activation(pe2[:], pdiff[:], ACT.Exp).then_inc(s["pe_done"], 1)
            act.wait_ge(s["xs_kept"], B)
            act.copy(rows[1][:, :, 0:D], rows[0][:, :, 0:D]).then_inc(s["rows1"], 1)

            def hidden(of):
                for u in range(2 * NCH):
                    i = u % 2
                    act.wait_ge(s["bT_ps"], of(2 * NCH, u + 1))
                    need(act, s["h_ps"], of(2 * NCH, u - 1))
                    act.copy(bT[i][:], bank[i][:, 0:CH]).then_inc(s["bT_out"], 1)
                    act.wait_ge(s["h_ps"], of(2 * NCH, u + 1))
                    need(act, s["hs_done"], of(2 * NCH, u - 1))
                    for half in range(2):
                        act.activation(hr[i][:, 2 * half:2 * half + 2, :],
                                       bank[2 + 2 * i + half][:].rearrange("p (f c) -> p f c", f=2),
                                       ACT.Relu).then_inc(s["hr_done"], 1)

            pairs(act, hidden)

        @block.vector
        def _(dve):
            def stage_a(g):
                dve.wait_ge(s["x_in"], g.times(4) * 4 + 16 if not g.known else 16)
                need(dve, s["mvA_done"], g.times(4))
                for t in range(G):
                    dve.bn_stats(stA[:, t, :], xr[:, bass.ds(g.times(4) + t, 1), :].rearrange("p o d -> p (o d)")
                                 ).then_inc(s["stA_done"], 1)
                need(dve, s["xnA_done"], g.times(4))
                dve.wait_ge(s["stA_done"], g.times(4, G))
                settle(dve)
                for t in range(G):
                    dve.bn_aggr(mvA[:, t, :], stA[:, t, :]).then_inc(s["mvA_done"], 1)
                dve.wait_ge(s["cT_ps"], g.times(1, 1))
                need(dve, s["v_ps"], g.times(1))
                dve.tensor_copy(cTA[:], bank[1][:]).then_inc(s["cT_out"], 1)
                dve.wait_ge(s["rstdA_done"], g.times(1, 1))
                need(dve, s["xT_ps"], g.times(1))
                for t in range(G):
                    dve.tensor_scalar(xnA[:, t, :], xr[:, bass.ds(g.times(4) + t, 1), :].rearrange("p o d -> p (o d)"),
                                      mvA[:, t, 0:1], rstdA[:, t:t + 1], ALU.subtract, ALU.mult
                                      ).then_inc(s["xnA_done"], 1)
                dve.wait_ge(s["v_ps"], g.times(1, 1))
                dve.tensor_tensor(v_all[:, bass.ds(g.times(4), G), :],
                                  bank[4][:].rearrange("p (g d) -> p g d", g=G),
                                  bv_all[:].unsqueeze(1).to_broadcast([P, G, D]), ALU.add).then_inc(s["v_out"], 1)
                dve.wait_ge(s["qf_done"], g.times(1, 1))
                dve.wait_ge(s["q1"], g.times(1, 1))
                need(dve, s["q3"], g.times(1))
                dve.tensor_tensor(qr[:], qf[:], qp[:, 0, :], ALU.subtract).then_inc(s["qr_done"], 1)
                dve.wait_ge(s["kf_done"], g.times(1, 1))
                dve.wait_ge(s["k1"], g.times(1, 1))
                need(dve, s["k3"], g.times(1))
                dve.tensor_tensor(kr[:], kf[:], kp[:, 0, :], ALU.subtract).then_inc(s["kr_done"], 1)
                dve.wait_ge(s["q2"], g.times(1, 1))
                need(dve, s["q_put"], _times96(dve, g))
                dve.tensor_tensor(qp[:, 2, :], qr[:], qp[:, 1, :], ALU.subtract).then_inc(s["q3"], 1)

            dve.wait_ge(s["b_in"], 64)
            groups(dve, stage_a)

            def maxes(b, c):
                dve.wait_ge(s["s1"], b.times(4, c + 1))
                if c == 0:
                    need(dve, s["n3"], b.times(1))
                dve.tensor_reduce(mxt[:, HC * c:HC * c + HC],
                                  bank[c % 2][:].rearrange("p (h k) -> p h k", h=HC), AX.X, ALU.max
                                  ).then_inc(s["mx"], 1)

            def normal_context(b):
                nat = bank[5][:].rearrange("p (h w) -> p h w", h=H)
                dve.wait_ge(s["nat"], b.times(1, 1))
                need(dve, s["cn_done"], b.times(1))
                dve.reciprocal(rden[:].unsqueeze(2), nat[:, :, DH:DH + 1]).then_inc(s["rec"], 1)
                need(dve, s["cnT_ps"], b.times(1))
                dve.wait_ge(s["rec"], b.times(1, 1))
                dve.tensor_tensor(cn[:].rearrange("p (h d) -> p h d", h=H), nat[:, :, 0:DH],
                                  rden[:].unsqueeze(2).to_broadcast([P, H, DH]), ALU.mult
                                  ).then_inc(s["cn_done"], 1)

            def top_two(b):
                logits = bank[7][:, 256:256 + E]
                dve.wait_ge(s["lg"], b.times(1, 1))
                need(dve, s["top_kept"], _twice(dve, b))
                settle(dve)
                dve.max(out=top8[:], in_=logits).then_inc(s["top_done"], 1)
                dve.wait_ge(s["top_done"], b.times(1, 1))
                settle(dve)
                dve.max_index(out=idx8[:], in_max=top8[:], in_values=logits).then_inc(s["idx_done"], 1)

            def residual(b):
                i = b.base % 2
                dve.wait_ge(s["wo_ps"], b.times(1, 1))
                need(dve, s["x1_kept"], b.times(1, -1))
                need(dve, s["xs_done"], b.times(1, -1))
                dve.tensor_tensor(x1[i][:].unsqueeze(1), bank[6][:, 128:256].unsqueeze(1),
                                  xr[:, bass.ds(b.times(1), 1), :], ALU.add).then_inc(s["x1_done"], 1)
                dve.wait_ge(s["x1_done"], b.times(1, 1))
                need(dve, s["mv_done"], b.times(1))
                dve.bn_stats(st[:], x1[i][:]).then_inc(s["st_done"], 1)
                dve.wait_ge(s["st_done"], b.times(1, 1))
                need(dve, s["xs_done"], b.times(1))
                settle(dve)
                dve.bn_aggr(mv[:], st[:]).then_inc(s["mv_done"], 1)

            def negative_max(b):
                need(dve, s["nT_ps"], b.times(1))
                dve.wait_ge(s["mx"], b.times(4, 4))
                dve.tensor_scalar(nparts[:, 0, :], mxt[:], -1.0, None, ALU.mult).then_inc(s["n1"], 1)
                dve.wait_ge(s["n1"], b.times(1, 1))
                dve.scalar_tensor_tensor(out=nrem[:], in0=mxt[:], scalar=-1.0, in1=nparts[:, 0, :],
                                         op0=ALU.mult, op1=ALU.subtract).then_inc(s["nr"], 1)
                dve.wait_ge(s["nr"], b.times(1, 1))
                dve.tensor_copy(nparts[:, 1, :], nrem[:]).then_inc(s["n2"], 1)
                dve.wait_ge(s["n2"], b.times(1, 1))
                dve.tensor_tensor(nparts[:, 2, :], nrem[:], nparts[:, 1, :], ALU.subtract).then_inc(s["n3"], 1)

            def normed(b):
                i = b.base % 2
                dve.wait_ge(s["rstd_done"], b.times(1, 1))
                need(dve, s["xsT_ps"], b.times(1, -1))
                need(dve, s["xs_kept"], b.times(1, -1))
                dve.tensor_scalar(xs[i][:], x1[i][:], mv[:, 0:1], rstd[:], ALU.subtract, ALU.mult
                                  ).then_inc(s["xs_done"], 1)

            dve.wait_ge(s["xbo"], NG)

            def step(j):
                b = j + 2
                if live(b):
                    maxes(b, 0)
                if live(j + (-1)):
                    normal_context(j + (-1))
                if live(b):
                    maxes(b, 1)
                if live(j + (-2)):
                    top_two(j + (-2))
                if live(b):
                    maxes(b, 2)
                if live(j + (-1)):
                    residual(j + (-1))
                if live(b):
                    maxes(b, 3)
                    negative_max(b)
                if live(j + (-1)):
                    normed(j + (-1))

            steps(dve, step, -2, 33)

            n = [32]

            def link(ins):
                n[0] += 1
                ins.then_inc(s["rt"], 1)
                dve.wait_ge(s["rt"], n[0])

            dve.wait_ge(s["top_kept"], 2 * B)
            link(dve.tensor_tensor(pdiff[:], tv[:, 1, :], tv[:, 0, :], ALU.subtract))
            tif = ti[:].rearrange("p k b -> p (k b)")
            link(dve.tensor_tensor(oh[:], tif.unsqueeze(2).to_broadcast([P, TOP_K * B, E]),
                                   ioE[:].unsqueeze(1).to_broadcast([P, TOP_K * B, E]), ALU.is_equal))
            dve.wait_ge(s["cnt_ps"], 1)
            link(dve.tensor_copy(cnt[:], bank[1][:].rearrange("p (t e) -> p e t", e=E)))
            link(dve.tensor_tensor_scan(cum[:].rearrange("p e t -> p (e t)"), seg[:].rearrange("p e t -> p (e t)"),
                                        cnt[:].rearrange("p e t -> p (e t)"), 0.0, ALU.mult, ALU.add))
            link(dve.tensor_tensor(cum[:], cum[:], cnt[:], ALU.subtract))
            link(dve.tensor_tensor(rk[:], bank[0][:].rearrange("p (t e) -> p t e", e=E),
                                   cum[:].rearrange("p e t -> p t e"), ALU.add))
            link(dve.tensor_tensor(rk[:], rk[:], oh[:], ALU.mult))
            link(dve.tensor_reduce(rank[:], rk[:], AX.X, ALU.add))
            vf = valid[:].rearrange("p k b -> p (k b)")
            link(dve.tensor_scalar(vf, rank[:], float(CAP), None, ALU.is_lt))
            link(dve.scalar_tensor_tensor(out=slot[:], in0=tif, scalar=float(CAP), in1=rank[:],
                                          op0=ALU.mult, op1=ALU.add))
            link(dve.scalar_tensor_tensor(out=rank[:], in0=vf, scalar=float(-FAR), in1=slot[:],
                                          op0=ALU.mult, op1=ALU.add))
            link(dve.tensor_scalar(sloti[:], rank[:], float(FAR), None, ALU.add))
            dve.wait_ge(s["xs_kept"], B)
            for k in range(TOP_K):
                dve.tensor_copy(rows[k][:, :, D:D + 1].bitcast(I32), ids[:, k, :].unsqueeze(2)
                                ).then_inc(s["rows1"], 1)
            dve.memset(rows[0][:, :, D + 1:RW], 0.0).then_inc(s["rows1"], 1)
            dve.memset(rows[1][:, :, D + 1:RW], 0.0).then_inc(s["rows1"], 1)
            dve.wait_ge(s["pe_done"], 1)
            link(dve.tensor_scalar(psumr[:], pe2[:], 1.0, None, ALU.add))
            link(dve.reciprocal(pdiff[:], psumr[:]))
            link(dve.tensor_tensor(prob[:, 0, :], pdiff[:], valid[:, 0, :], ALU.mult))
            link(dve.tensor_tensor(pe2[:], pe2[:], pdiff[:], ALU.mult))
            link(dve.tensor_tensor(prob[:, 1, :], pe2[:], valid[:, 1, :], ALU.mult))

            def squares(of):
                for u in range(2 * NCH):
                    i = u % 2
                    dve.wait_ge(s[f"br_in{i}"], of(16 * NCH, 16 * (u // 2 + 1)))
                    need(dve, s[f"put{i}"], of(32 * NCH, 32 * (u // 2)))
                    dve.tensor_copy(dst[i][:].unsqueeze(2), br[i][:, :, D:D + 1].bitcast(I32)
                                    ).then_inc(s["dst_done"], 1)
                    dve.wait_ge(s["hr_done"], of(4 * NCH, 2 * u + 2))
                    need(dve, s["y_ps"], of(2 * NCH, u - 1))
                    dve.tensor_tensor(hs[i], hr[i], hr[i], ALU.mult).then_inc(s["hs_done"], 1)
                    dve.wait_ge(s["y_ps"], of(2 * NCH, u + 1))
                    dve.tensor_copy(ys[i][:], bank[6 + i][:, 0:CH].rearrange("p (t d) -> p t d", t=2)
                                    ).then_inc(s["y_out"], 1)

            pairs(dve, squares)

            for g in range(NG):
                y = ya[g % 2]
                dve.wait_ge(s[f"ya_in{g % 2}"], 32 * (g // 2 + 1))
                for t in range(G):
                    b = G * g + t
                    dve.scalar_tensor_tensor(out=xr[:, b, :], in0=y[0][:, t, :], scalar=prob[:, 0, b:b + 1],
                                             in1=xr[:, b, :], op0=ALU.mult, op1=ALU.add).then_inc(s["e1"], 1)
                for t in range(G):
                    b = G * g + t
                    dve.wait_ge(s["e1"], b + 1)
                    dve.scalar_tensor_tensor(out=xr[:, b, :], in0=y[1][:, t, :], scalar=prob[:, 1, b:b + 1],
                                             in1=xr[:, b, :], op0=ALU.mult, op1=ALU.add).then_inc(s["e2"], 1)

        @block.tensor
        def _(pe):
            pe.wait_ge(s["wperm"], 4)
            pe.wait_ge(s["c_ready"], 1)
            for i in range(2):
                pe.matmul(bank[7][:, i:i + 1], bqk_row[0:1, i, :], ident[0:1, 0:1], start=True, stop=True
                          ).then_inc(s["bcol_ps"], 1)
            pe.wait_ge(s["g_in"], 16)
            pe.transpose(bank[7][:, 8:8 + E], wg_raw[:], ident[0:E, 0:E]).then_inc(s["wgT_ps"], 1)

            def stage_a(g):
                pe.wait_ge(s["c_inn"], g.times(4) * 4 + 16 if not g.known else 16)
                need(pe, s["cT_out"], g.times(1))
                for t in range(G):
                    mm = pe.transpose(bank[1][:, t * S:(t + 1) * S], c_in[:, t, :], ident[:])
                mm.then_inc(s["cT_ps"], 1)
                pe.wait_ge(s["xnA_done"], g.times(4, G))
                need(pe, s["xT_out"], g.times(1))
                for t in range(G):
                    mm = pe.transpose(bank[0][:, t * S:(t + 1) * S], xnA[:, t, :], ident[:])
                mm.then_inc(s["xT_ps"], 1)
                pe.wait_ge(s["cT_out"], g.times(1, 1))
                need(pe, s["k1"], g.times(1))
                pe.matmul(bank[3][:], wk_s[:], cTA[:], start=True, stop=True).then_inc(s["k_ps"], 1)
                need(pe, s["v_out"], g.times(1))
                for t in range(G):
                    mm = pe.matmul(bank[4][:, t * D:(t + 1) * D], cTA[:, t * S:(t + 1) * S], wv_s[:],
                                   start=True, stop=True)
                mm.then_inc(s["v_ps"], 1)
                pe.wait_ge(s["xT_out"], g.times(1, 1))
                need(pe, s["q1"], g.times(1))
                pe.matmul(bank[2][:], wq_s[:], xTA[:], start=True, stop=True).then_inc(s["q_ps"], 1)

            groups(pe, stage_a)
            pe.wait_ge(s["q1"], NG)
            pe.wait_ge(s["k1"], NG)
            pe.wait_ge(s["v_out"], NG)
            pe.wait_ge(s["bcol"], 3)

            def scores_for_max(b, c):
                i = b.base % 4
                if c == 0:
                    pe.wait_ge(q_in[i], b.rounds16())
                    pe.wait_ge(km_in[i], b.rounds16())
                need(pe, s["mx"], b.times(4, c - 1))
                for h in range(HC):
                    cols = slice((HC * c + h) * S, (HC * c + h + 1) * S)
                    mm = pe.matmul(bank[c % 2][:, h * S:(h + 1) * S], qs[i][:, cols], km[i][:, cols],
                                   start=True, stop=True)
                mm.then_inc(s["s1"], 1)

            def scores_for_exp(b, c):
                i = b.base % 4
                if c == 0:
                    pe.wait_ge(k_in[i], b.rounds16(16))
                    pe.wait_ge(m_in[i], b.rounds16())
                need(pe, s["ex"], b.times(4, c - 1))
                for h in range(HC):
                    cols = slice((HC * c + h) * S, (HC * c + h + 1) * S)
                    mm = pe.matmul(bank[2 + c % 2][:, h * S:(h + 1) * S], ks[i][:, cols], qs[i][:, cols],
                                   start=True, stop=True)
                mm.then_inc(s["s2"], 1)

            def times_v(b, c):
                pe.wait_ge(s["ex"], b.times(4, c + 1))
                if c == 0:
                    pe.wait_ge(s["va_in"], b.times(1, 1))
                    need(pe, s["av_out"], b.times(1))
                for h in range(HC):
                    mm = pe.matmul(bank[4][VW * h:VW * (h + 1), c * S:(c + 1) * S],
                                   va[b.base % 2][:, HC * c + h, :], pr[c][:, h * S:(h + 1) * S],
                                   start=True, stop=True, tile_position=(0, VW * h))
                mm.then_inc(s["av"], 1)

            def context_back(b):
                pe.wait_ge(s["av_out"], b.times(1, 1))
                need(pe, s["cn_done"], b.times(1))
                for c in range(NC):
                    mm = pe.transpose(bank[5][:, c * S:(c + 1) * S], avs[:, c * S:(c + 1) * S], ident[:])
                mm.then_inc(s["nat"], 1)

            def context_turned(b):
                pe.wait_ge(s["cn_done"], b.times(1, 1))
                need(pe, s["x1_done"], b.times(1))
                pe.transpose(bank[6][:, 0:128], cn[:], ident[:]).then_inc(s["cnT_ps"], 1)

            def output_rows(b):
                pe.wait_ge(s["cnT_out"], b.times(1, 1))
                pe.matmul(bank[6][:, 128:256], cnT[:], wo_s[:], start=True, stop=True).then_inc(s["wo_ps"], 1)

            def maxima_turned(b):
                pe.wait_ge(s["n3"], b.times(1, 1))
                need(pe, s["idx_done"], b.times(1, -3))
                pe.transpose(bank[7][:, 0:S // 2].bitcast(BF16), nparts_pad[:], identb[:]).then_inc(s["nT_ps"], 1)

            def normed_turned(b):
                pe.wait_ge(s["xs_done"], b.times(1, 1))
                pe.wait_ge(s["nT_out"], min(b.base + 4, B) if b.known else b.times(1, 4))
                need(pe, s["idx_done"], b.times(1))
                pe.transpose(bank[7][:, 128:256], xs[b.base % 2][:], ident[:]).then_inc(s["xsT_ps"], 1)

            def logits(b):
                pe.wait_ge(s["xsT_out"], b.times(1, 1))
                pe.matmul(bank[7][:, 256:256 + E], xsT[:], wgT[:], start=True, stop=True).then_inc(s["lg"], 1)

            def step(j):
                ahead, now, last, second = j + 2, j, j + (-1), j + (-2)
                for c in range(NC):
                    if live(ahead):
                        scores_for_max(ahead, c)
                    if c == 0 and live(j + 1):
                        maxima_turned(j + 1)
                    if live(now):
                        scores_for_exp(now, c)
                        if c:
                            times_v(now, c - 1)
                    if c == 0 and live(second):
                        normed_turned(second)
                    if c == 0 and live(last):
                        context_back(last)
                    if c == 1 and live(second):
                        logits(second)
                    if c == 1 and live(last):
                        context_turned(last)
                    if c == 2 and live(last):
                        output_rows(last)
                if live(now):
                    times_v(now, NC - 1)

            steps(pe, step, -2, 33)

            pe.wait_ge(s["rt"], 34)
            ohf = oh[:].rearrange("p t e -> p (t e)")
            pe.matmul(bank[0][:], before[:], ohf, start=True, stop=True).then_inc(s["rk_ps"], 1)
            pe.matmul(bank[1][:], onesb[:], ohf, start=True, stop=True).then_inc(s["cnt_ps"], 1)
            pe.wait_ge(s["rt"], 32 + 6)

            def chunks(of):
                def turn(u):
                    i = u % 2
                    pe.wait_ge(s[f"br_in{i}"], of(16 * NCH, 16 * (u // 2 + 1)))
                    need(pe, s["bT_out"], of(2 * NCH, u - 1))
                    for t in range(2):
                        mm = pe.transpose(bank[i][:, t * P:(t + 1) * P], br[i][:, t, 0:D], ident[:])
                    mm.then_inc(s["bT_ps"], 1)

                def up(u):
                    i = u % 2
                    w = w1[u // NCH]
                    if u % NCH == 0:
                        pe.wait_ge(s[f"w_in{u // NCH}"], of(32, 32))
                    pe.wait_ge(s["bT_out"], of(2 * NCH, u + 1))
                    need(pe, s["hr_done"], of(4 * NCH, 2 * u - 2))
                    for f in range(NF):
                        mm = pe.matmul(bank[2 + 2 * i + f // 2][:, (f % 2) * CH:(f % 2 + 1) * CH],
                                       w[:, f * P:(f + 1) * P], bT[i][:], start=True, stop=True)
                    mm.then_inc(s["h_ps"], 1)

                def down(u):
                    i = u % 2
                    w = w2[u // NCH]
                    pe.wait_ge(s["hs_done"], of(2 * NCH, u + 1))
                    need(pe, s["y_out"], of(2 * NCH, u - 1))
                    for t in range(2):
                        for f in range(NF):
                            mm = pe.matmul(bank[6 + i][:, t * D:(t + 1) * D], hs[i][:, f, t * P:(t + 1) * P],
                                           w[:, f, :], start=(f == 0), stop=(f == NF - 1))
                    mm.then_inc(s["y_ps"], 1)

                turn(0)
                for u in range(2 * NCH):
                    if u + 1 < 2 * NCH:
                        turn(u + 1)
                    up(u)
                    if u:
                        down(u - 1)
                down(2 * NCH - 1)

            pairs(pe, chunks)


_INS = ['x', 'ctx_1024', 'L0_xattn_Wq', 'L0_xattn_bq', 'L0_xattn_Wk', 'L0_xattn_bk', 'L0_xattn_Wv', 'L0_xattn_bv',
        'L0_xattn_Wo', 'L0_xattn_bo', 'L0_ffn_w_g', 'L0_ffn_c_fc', 'L0_ffn_c_proj']
_OUT = ((32, 128, 128), 'float32')


def kernel(**inputs):
    import numpy as np
    import concourse.bacc as bacc
    from concourse.bass_utils import run_bass_kernel_spmd as run

    nc = bacc.Bacc("TRN2", target_bir_lowering=False, num_devices=1)
    arrays, args = {}, []
    for name in _INS:
        a = np.ascontiguousarray(inputs[name])
        arrays[f"in_{name}"] = a
        args.append(nc.dram_tensor(f"in_{name}", a.shape, mybir.dt.from_np(a.dtype), kind="ExternalInput").ap())
    shape, dtype = _OUT
    args.append(nc.dram_tensor("out_0", shape, mybir.dt.from_np(np.dtype(dtype)), kind="ExternalOutput").ap())
    xattn_moe_kernel(nc, *args)
    r = run(nc, [arrays], core_ids=[0])
    return r.results[0]["out_0"]
```

```python
from contextlib import ExitStack

import concourse.bass as bass
from concourse import mybir

ALU = mybir.AluOpType
ACT = mybir.ActivationFunctionType
AX = mybir.AxisListType
F32 = mybir.dt.float32
BF16 = mybir.dt.bfloat16
I32 = mybir.dt.int32
U32 = mybir.dt.uint32

P = 128
Q_TERMS = (0, 1, 2, 0, 1, 0)
K_TERMS = (0, 0, 0, 1, 1, 2)
EPS = 1e-5
TOP_K = 2


class At:

    def __init__(self, base, regs=None, mult=4):
        self.base, self.regs, self.mult = base, regs, mult

    def times(self, k, plus=0):
        const = k * self.base + plus
        return const if self.regs is None else self.regs[k * self.mult] + const

    def rounds16(self, plus=0):
        const = 16 * (self.base // 4 + 1) + plus
        return const if self.regs is None else self.regs[16] + const

    def __add__(self, n):
        return At(self.base + n, self.regs, self.mult)

    @property
    def known(self):
        return self.regs is None


def xattn_moe_kernel(nc, x, ctx, Wq, bq, Wk, bk, Wv, bv, Wo, bo, w_g, c_fc, c_proj, out):
    B, S, D = x.shape
    E, _, F = c_fc.shape
    H = 16
    DH = D // H
    NF = F // P
    N = B * S
    CAP = int(1.25 * N * TOP_K / E)
    G = 4
    NG = B // G
    NT = len(Q_TERMS)
    KR = NT * DH
    KC = 96
    HC = 4
    NC = H // HC
    VW = 32
    RW = 132
    CH = 256
    NCH = CAP // CH
    SCALE = 1.0 / float(DH) ** 0.5
    FAR = 100000
    LO, HI = 2, NG - 3
    assert S == P and D == P and E == 8 and CAP % CH == 0 and B % 4 == 0

    def dram(name, shape, dt):
        return nc.dram_tensor(name, shape, dt, kind="Internal").ap()

    q_stack_d = dram("q_stack_d", (B, NT, P, S), BF16)
    k_stack_d = dram("k_stack_d", (B, NT, P, S), BF16)
    negmax_d = dram("negmax_d", (B, 3, H * S), BF16)
    slots_d = dram("slots_d", (E * CAP, RW), F32)
    result_d = dram("result_d", (TOP_K * N, D), F32)

    with ExitStack() as es:
        def sb(name, shape, dt=F32):
            return es.enter_context(nc.sbuf_tensor(name, shape, dt))

        def sem(name):
            return es.enter_context(nc.semaphore(name))

        bank = [es.enter_context(nc.psum_tensor(f"bank{i}", [P, 512], F32)) for i in range(8)]

        ident = sb("ident", [P, P])
        identb = sb("identb", [P, P], BF16)
        before = sb("before", [P, P], BF16)
        onesb = sb("onesb", [P, P], BF16)
        ones_rows = sb("ones_rows", [3, H * S], BF16)
        ioE = sb("ioE", [P, E])
        seg = sb("seg", [P, E, B])
        ids = sb("ids", [P, TOP_K, B], I32)
        mhalf = sb("mhalf", [P, G])
        one_g = sb("one_g", [P, G])
        cap_g = sb("cap_g", [P, G])
        wq_raw = sb("wq_raw", [P, D])
        wk_raw = sb("wk_raw", [P, D])
        wq_s = sb("wq_s", [P, D])
        wk_s = sb("wk_s", [P, D])
        wv_s = sb("wv_s", [P, D])
        wo_s = sb("wo_s", [P, D])
        carry = sb("carry", [P, E])
        bqk_raw = sb("bqk_raw", [1, 2, D])
        bqk_row = sb("bqk_row", [1, 2, D])
        bq_col = sb("bq_col", [P, 1])
        bk_col = sb("bk_col", [P, 1])
        bv_all = sb("bv_all", [P, D])
        bo_all = sb("bo_all", [P, D])
        wg_raw = sb("wg_raw", [E, D])
        wgT = sb("wgT", [P, E])
        empty = sb("empty", [P, 4, RW])
        zeros = sb("zeros", [P, 4, D])

        xr = sb("xr", [P, B, D])
        c_in = sb("c_in", [P, G, D])
        v_all = sb("v_all", [P, B, D])
        stA = sb("stA", [P, G, 6])
        mvA = sb("mvA", [P, G, 2])
        vareA = sb("vareA", [P, G])
        rstdA = sb("rstdA", [P, G])
        xnA = sb("xnA", [P, G, D])
        xTA = sb("xTA", [P, G * S])
        cTA = sb("cTA", [P, G * S])
        qf = sb("qf", [P, G * S])
        kf = sb("kf", [P, G * S])
        qr = sb("qr", [P, G * S])
        kr = sb("kr", [P, G * S])
        qp = sb("qp", [P, 3, G * S], BF16)
        kp = sb("kp", [P, 3, G * S], BF16)

        qs = [sb(f"qs{i}", [KC, H * S], BF16) for i in range(4)]
        ks = [sb(f"ks{i}", [KC, H * S], BF16) for i in range(4)]
        km = [sb(f"km{i}", [KC, H * S], BF16) for i in range(4)]
        va = [sb(f"va{i}", [P, H, VW]) for i in range(2)]
        mxt = sb("mxt", [P, H])
        nrem = sb("nrem", [P, H])
        nparts_pad = sb("nparts_pad", [P, P], BF16)
        nparts = nparts_pad[:, 0:3 * H].rearrange("p (t h) -> p t h", t=3)
        nT = [sb(f"nT{i}", [3 * H, S], BF16) for i in range(4)]
        pr = [sb(f"pr{i}", [P, HC * S]) for i in range(4)]
        avs = sb("avs", [P, NC * S])
        rden = sb("rden", [P, H])
        cn = sb("cn", [P, D])
        cnT = sb("cnT", [P, S])
        x1 = [sb(f"x1_{i}", [P, D]) for i in range(2)]
        st = sb("st", [P, 6])
        mv = sb("mv", [P, 2])
        vare = sb("vare", [P, 1])
        rstd = sb("rstd", [P, 1])
        xs = [sb(f"xs{i}", [P, D]) for i in range(2)]
        xsT = sb("xsT", [P, S])
        top8 = sb("top8", [P, E])
        idx8 = sb("idx8", [P, E], U32)
        rows = sb("rows", [P, B, RW])

        tv = sb("tv", [P, TOP_K, B])
        ti = sb("ti", [P, TOP_K, B])
        ohg = sb("ohg", [P, G, E], BF16)
        rkg = sb("rkg", [P, G, E])
        rkm = sb("rkm", [P, G, E])
        rankg = sb("rankg", [P, G])
        skip = sb("skip", [P, G])
        slotg = sb("slotg", [P, G])
        slotig = [sb(f"slotig{i}", [P, G], I32) for i in range(2)]
        stage = sb("stage", [P, G, RW])
        oh = sb("oh", [P, B, E], BF16)
        cnt = sb("cnt", [P, E, B])
        cum = sb("cum", [P, E, B])
        rk = sb("rk", [P, B, E])
        rank = sb("rank", [P, B])
        valid = sb("valid", [P, TOP_K, B])
        slot = sb("slot", [P, B])
        sloti = sb("sloti", [P, B], I32)
        pdiff = sb("pdiff", [P, B])
        pe2 = sb("pe2", [P, B])
        psumr = sb("psumr", [P, B])
        prob = sb("prob", [P, TOP_K, B])

        w1 = [sb(f"w1_{i}", [P, F]) for i in range(2)]
        w2 = [sb(f"w2_{i}", [P, NF, D]) for i in range(2)]
        br = [sb(f"br{i}", [P, 2, RW]) for i in range(NCH)]
        bT = [sb(f"bT{i}", [P, CH]) for i in range(2)]
        ys = [sb(f"ys{i}", [P, 2, D]) for i in range(NCH)]
        room = v_all[:].rearrange("p b d -> p (b d)").rearrange("p (i f c) -> p i f c", i=4, f=NF)
        hr = [room[:, i] for i in range(2)]
        hs = [room[:, 2 + i] for i in range(2)]

        ya = [[xTA, cTA], [qf, kf]]
        ya = [[t[:].rearrange("p (g d) -> p g d", g=G) for t in pair] for pair in ya]

        names = """w_in b_in g_in c_ready e_ready wperm bcol bcol_ps wgT_ps fills rfills zeroed empty0
            x_in0 x_in1 x_in2 c_inn stA_done mvA_done vareA_done rstdA_done xnA_done xbo
            xT_ps cT_ps xT_out cT_out q_ps k_ps v_ps qf_done kf_done q1 k1 qr_done kr_done q2 k2 q3 k3
            v_out q_put k_put
            s1 mx n1 nr n2 n3 nT_ps nT_out s2 ex av va_in av_out nat rec cn_done cnT_ps cnT_out wo_ps x1_done
            st_done mv_done vare_done rstd_done xs_done x1_kept xs_kept xsT_ps xsT_out lg top_done idx_done
            top_kept ohg_done rkg_ps rkg_done carried rkm_done rankg_done validg skipg slotg_done slotig_done
            staged gdone sc1
            rt rt2 cnt_ps pe_done rows2 sc2
            w_in0 w_in1 bT_ps bT_out h_ps hr_done hs_done y_ps y_out
            ya_in0 ya_in1 e1 e2 out_put0 out_put1 settled""".split()
        s = {n: sem(n) for n in names}
        q_in = [sem(f"q_in{i}") for i in range(4)]
        k_in = [sem(f"k_in{i}") for i in range(4)]
        km_in = [sem(f"km_in{i}") for i in range(4)]
        m_put = [sem(f"m_put{i}") for i in range(4)]
        m_in = [sem(f"m_in{i}") for i in range(4)]
        br_in = [sem(f"br_in{i}") for i in range(NCH)]
        put = [sem(f"put{i}") for i in range(NCH)]

        def need(eng, what, value):
            if not isinstance(value, int) or value > 0:
                eng.wait_ge(what, value)

        def settle(eng):
            eng.sem_inc(s["settled"], 1)

        def steps(eng, body, keys=()):
            for j in range(-2, LO * G):
                body(At(j), j % G, At(j // G, mult=1))
            with eng.Fori(LO, HI) as r:
                regs = {1: r, 4: eng.snap(r * 4), 16: eng.snap(r * 16)}
                for k in keys:
                    regs[k] = eng.snap(r * k)
                for u in range(G):
                    body(At(u, regs), u, At(0, regs, 1))
            for j in range(HI * G, B + 4):
                body(At(j), j % G, At(j // G, mult=1))

        def group_of(r):
            g = r + 2
            return g if not g.known or 2 <= g.base < NG else None

        def ranked(r):
            q = r + (-1)
            return q if not q.known or 0 <= q.base < NG else None

        def pairs(eng, body):
            body(lambda k, plus: plus)
            with eng.Fori(1, E // 2) as pair:
                held = {}

                def of(k, plus):
                    if k not in held:
                        held[k] = eng.snap(pair * k)
                    return held[k] + plus

                for k in (2 * NCH, 64, 4 * NCH, 32, 2):
                    of(k, 0)
                body(of)

        def live(b):
            return not b.known or 0 <= b.base < B

        def next_expert(eng, of, plus):
            e = of(2, plus)
            return e % E if isinstance(e, int) else eng.snap(e % E)

        def _twice(eng, b):
            return 2 * b.base if b.known else b.times(1) * 2

        block = es.enter_context(nc.Block())

        @block.sync
        def _(sp):
            for w, d in ((wq_raw, Wq), (wk_raw, Wk), (wv_s, Wv), (wo_s, Wo)):
                sp.dma_start(w[:], d).then_inc(s["w_in"], 16)
            sp.dma_start(bqk_raw[:, 0, :], bq.unsqueeze(0)).then_inc(s["b_in"], 16)
            sp.dma_start(bqk_raw[:, 1, :], bk.unsqueeze(0)).then_inc(s["b_in"], 16)
            sp.dma_start(bv_all[:], bv.partition_broadcast(P)).then_inc(s["b_in"], 16)
            sp.dma_start(bo_all[:], bo.partition_broadcast(P)).then_inc(s["b_in"], 16)
            sp.dma_start(wg_raw[:], w_g).then_inc(s["g_in"], 16)

            xg = x.rearrange("b s d -> s b d")
            cg = ctx.rearrange("b s d -> s b d")

            def load_ctx(g):
                need(sp, s["cT_ps"], g.times(1))
                sp.dma_start(c_in[:], cg[:, bass.ds(g.times(4), G), :]).then_inc(s["c_inn"], 16)

            load_ctx(At(0, mult=1))
            for i, (b0, b1) in enumerate(((0, G), (G, 2 * G), (2 * G, B))):
                sp.dma_start(xr[:, b0:b1, :], xg[:, b0:b1, :]).then_inc(s[f"x_in{i}"], 16)

            sp.wait_ge(s["e_ready"], 1)
            slot_quarters = slots_d.rearrange("(q p a b) w -> q p a (b w)", q=4, p=P, b=4)
            for q in range(4):
                sp.dma_start(slot_quarters[q],
                             empty[:].rearrange("p b w -> p (b w)").unsqueeze(1)
                             .to_broadcast([P, E * CAP // P // 16, 4 * RW])).then_inc(s["fills"], 16)

            def store(g, parts, stack, done, put_, terms, which):
                if which[0] == 0:
                    for part in done:
                        need(sp, s[part], g.times(1, 1))
                for t in which:
                    sp.dma_start(stack[bass.ds(g.times(4), G), t, :, :].rearrange("b r q -> r b q"),
                                 parts[:, terms[t], :].rearrange("p (b q) -> p b q", b=G)
                                 ).then_inc(s[put_], 16)

            def store_k(g, which):
                store(g, kp, k_stack_d, ("k1", "k2", "k3"), "k_put", K_TERMS, which)

            def store_q(g, which):
                store(g, qp, q_stack_d, ("q1", "q2", "q3"), "q_put", Q_TERMS, which)

            for g in range(2):
                load_ctx(At(g + 1, mult=1))
                store_k(At(g, mult=1), range(NT))
                store_q(At(g, mult=1), range(NT))
            sp.wait_ge(s["c_ready"], 1)
            for i in range(4):
                sp.dma_start(ks[i][KR:KR + 3, :], ones_rows[:]).then_inc(k_in[i], 16)

            def load_stacks(b, u, r):
                if not live(b):
                    return
                i = b.base % 4
                if u == 1 or b.known and b.base == 0:
                    g = r + 1
                    sp.wait_ge(s["q_put"], g.times(16 * NT, 16 * NT))
                    settle(sp)
                    sp.wait_ge(s["k_put"], g.times(16 * NT, 16 * NT))
                    settle(sp)
                need(sp, s["s2"], b.times(4, -12))
                row = bass.ds(b.times(1), 1)
                for t, src, got in ((qs, q_stack_d, q_in), (km, k_stack_d, km_in), (ks, k_stack_d, k_in)):
                    sp.dma_start(t[i][0:KR, :], src[row].rearrange("o t (d h) q -> (o t d) (h q)", d=DH)
                                 ).then_inc(got[i], 16)

            def max_rows(b):
                if not live(b):
                    return
                i = b.base % 4
                sp.wait_ge(m_put[i], b.rounds16())
                sp.dma_start(qs[i][KR:KR + 3, :], negmax_d[bass.ds(b.times(1), 1)].rearrange("o t r -> (o t) r")
                             ).then_inc(m_in[i], 16)

            load_stacks(At(0), 0, At(-1, mult=1))
            load_stacks(At(1), 0, None)
            res_parts = result_d.rearrange("(q p a b) d -> q p a (b d)", q=NG, p=P, b=4)

            def step(j, u, r):
                if not (j.known and j.base < -1):
                    load_stacks(j + 3, u, r)
                max_rows(j + 1)
                g, before_g = group_of(r), group_of(r + (-1))
                if u == 0 and before_g is not None:
                    store_q(before_g, range(NT))
                if u == 1 and g is not None and not (g.known and g.base >= NG - 1):
                    load_ctx(g + 1)
                if u == 3 and g is not None:
                    store_k(g, range(NT))
                if u == 2 and (not r.known or 0 <= r.base < NG):
                    sp.dma_start(res_parts[bass.ds(r.times(1), 1)].rearrange("o p a w -> (o p) a w"),
                                 zeros[:].rearrange("p b w -> p (b w)").unsqueeze(1)
                                 .to_broadcast([P, TOP_K * N // P // 4 // NG, 4 * D])).then_inc(s["rfills"], 16)

            steps(sp, step, (16 * NT,))

            def load_weights(e, i):
                sp.dma_start(w1[i][:], c_fc[bass.ds(e, 1)].rearrange("o c f -> (o c) f")).then_inc(s[f"w_in{i}"], 16)
                sp.dma_start(w2[i][:], c_proj[bass.ds(e, 1)].rearrange("o (n f) c -> (o f) n c", n=NF)
                             ).then_inc(s[f"w_in{i}"], 16)

            load_weights(0, 0)
            load_weights(1, 1)
            sp.wait_ge(s["sc1"], 16 * B)
            sp.wait_ge(s["sc2"], 16 * B)
            slot_rows = slots_d.rearrange("(n t p) w -> n p t w", t=2, p=P)

            def chunks(of):
                for u in range(2 * NCH):
                    need(sp, put[u % NCH], of(64, 32 * (u // NCH)))
                    sp.dma_start(br[u % NCH][:],
                                 slot_rows[bass.ds(of(2 * NCH, u), 1)].rearrange("o p t w -> (o p) t w")
                                 ).then_inc(br_in[u % NCH], 16)
                    if u == 1 and not isinstance(of(2, 0), int):
                        e = next_expert(sp, of, 1)
                        sp.wait_ge(s["y_ps"], of(2 * NCH, 0))
                        load_weights(e, 1)
                    if u == NCH + 1:
                        e = next_expert(sp, of, 2)
                        sp.wait_ge(s["y_ps"], of(2 * NCH, NCH))
                        load_weights(e, 0)

            pairs(sp, chunks)
            sp.wait_ge(s["w_in0"], 32 * (E // 2 + 1))
            sp.wait_ge(s["w_in1"], 32 * (E // 2))

            for i in range(NCH):
                sp.wait_ge(put[i], 32 * E)
            res = result_d.rearrange("(k g t p) d -> k g p t d", k=TOP_K, t=G, p=P)
            outg = out.rearrange("(g t) s d -> g s t d", t=G)
            for g in range(NG + 1):
                if g < NG:
                    need(sp, s["e2"], G * (g - 1))
                    for k in range(TOP_K):
                        sp.dma_start(ya[g % 2][k], res[k, g]).then_inc(s[f"ya_in{g % 2}"], 16)
                if g >= 1:
                    sp.wait_ge(s["e2"], G * g)
                    sp.dma_start(outg[g - 1], xr[:, G * (g - 1):G * g, :]).then_inc(s[f"out_put{g % 2}"], 16)
            sp.wait_ge(s["out_put0"], 16 * NG // 2)
            sp.wait_ge(s["out_put1"], 16 * NG // 2)

        @block.gpsimd
        def _(pool):
            pool.memset(ident[:], 0.0).then_inc(s["rt"], 1)
            pool.memset(mhalf[:], -0.5).then_inc(s["rt"], 1)
            pool.wait_ge(s["empty0"], 1)
            pool.iota(empty[:, :, D:D + 1].bitcast(I32), [[0, 4], [0, 1]], base=TOP_K * N + FAR % 8192,
                      channel_multiplier=0).then_inc(s["e_ready"], 1)
            pool.wait_ge(s["rt"], 2)
            pool.affine_select(out=ident[:], in_=ident[:], compare_op=ALU.not_equal, fill=1.0, base=0,
                               pattern=[[-1, P]], channel_multiplier=1).then_inc(s["rt"], 1)
            pool.wait_ge(s["w_in"], 64)
            pool.wait_ge(s["b_in"], 64)
            for w, r in ((wk_s, wk_raw), (wq_s, wq_raw)):
                pool.tensor_copy(w[:].rearrange("p (d h) -> p d h", d=DH),
                                 r[:].rearrange("p (h d) -> p d h", d=DH)).then_inc(s["wperm"], 1)
            for i in range(2):
                pool.tensor_copy(bqk_row[:, i, :].rearrange("p (d h) -> p d h", d=DH),
                                 bqk_raw[:, i, :].rearrange("p (h d) -> p d h", d=DH)).then_inc(s["wperm"], 1)
            pool.wait_ge(s["rt"], 3)
            pool.tensor_copy(identb[:], ident[:]).then_inc(s["rt"], 1)
            pool.memset(ones_rows[:], 1.0).then_inc(s["rt"], 1)
            pool.wait_ge(s["rt"], 5)
            pool.sem_inc(s["c_ready"], 1)

            def deviations(g):
                pool.wait_ge(s["mvA_done"], g.times(4, G))
                need(pool, s["rstdA_done"], g.times(1))
                settle(pool)
                pool.tensor_scalar(vareA[:], mvA[:, :, 1], EPS, None, ALU.add).then_inc(s["vareA_done"], 1)
                pool.wait_ge(s["vareA_done"], g.times(1, 1))
                need(pool, s["xnA_done"], g.times(4))
                pool.tensor_tensor(rstdA[:], vareA[:], mhalf[:], ALU.pow).then_inc(s["rstdA_done"], 1)

            def add_bias(g):
                pool.wait_ge(s["xnA_done"], g.times(4, G))
                xg = xr[:, bass.ds(g.times(4), G), :]
                pool.tensor_tensor(xg, xg, bo_all[:].unsqueeze(1).to_broadcast([P, G, D]), ALU.add
                                   ).then_inc(s["xbo"], 1)

            def third_k(g):
                pool.wait_ge(s["k2"], g.times(1, 1))
                need(pool, s["k_put"], g.times(16 * NT))
                pool.tensor_tensor(kp[:, 2, :], kr[:], kp[:, 1, :], ALU.subtract).then_inc(s["k3"], 1)

            def third_q(g):
                pool.wait_ge(s["q2"], g.times(1, 1))
                need(pool, s["q_put"], g.times(16 * NT))
                pool.tensor_tensor(qp[:, 2, :], qr[:], qp[:, 1, :], ALU.subtract).then_inc(s["q3"], 1)

            deviations(At(0, mult=1))
            add_bias(At(0, mult=1))
            deviations(At(1, mult=1))
            add_bias(At(1, mult=1))
            for g in range(2):
                third_k(At(g, mult=1))
                third_q(At(g, mult=1))
            deviations(At(2, mult=1))

            pool.memset(before[:], 1.0).then_inc(s["rt"], 1)
            pool.memset(seg[:], 1.0).then_inc(s["rt"], 1)
            pool.memset(onesb[:], 1.0).then_inc(s["rt"], 1)
            pool.memset(one_g[:], 1.0).then_inc(s["rt"], 1)
            pool.memset(cap_g[:], float(CAP)).then_inc(s["rt"], 1)
            pool.memset(carry[:], 0.0).then_inc(s["rt"], 1)
            pool.memset(rows[:, :, D + 1:RW], 0.0).then_inc(s["rt"], 1)
            pool.iota(ids[:], [[N, TOP_K], [P, B]], base=0, channel_multiplier=1).then_inc(s["rt"], 1)
            pool.iota(ioE[:], [[1, E]], base=0, channel_multiplier=0,
                      allow_small_or_imprecise_dtypes=True).then_inc(s["rt"], 1)
            pool.wait_ge(s["rt"], 14)
            pool.affine_select(out=before[:], in_=before[:], compare_op=ALU.is_gt, fill=0.0, base=0,
                               pattern=[[1, P]], channel_multiplier=-1).then_inc(s["rt"], 1)
            pool.memset(seg[:, :, 0:1], 0.0).then_inc(s["rt"], 1)
            pool.tensor_copy(rows[:, :, D:D + 1].bitcast(I32), ids[:, 0, :].unsqueeze(2)).then_inc(s["rt"], 1)
            pool.wait_ge(s["rt"], 17)
            pool.wait_ge(s["fills"], 64)
            pool.sem_inc(s["c_ready"], 1)

            def v_beside_ones(b):
                if not live(b):
                    return
                pool.wait_ge(s["v_out"], (b.base // G + 1) if b.known else b.regs[1] + (b.base // G + 1))
                need(pool, s["av"], b.times(4, -4))
                if b.known and b.base < 2:
                    pool.wait_ge(s["zeroed"], 17)
                pool.tensor_copy(va[b.base % 2][:, :, 0:DH],
                                 v_all[:, bass.ds(b.times(1), 1), :].rearrange("p o (h d) -> p (o h) d", d=DH)
                                 ).then_inc(s["va_in"], 1)

            def keep_normed(b):
                if not live(b):
                    return
                pool.wait_ge(s["xs_done"], b.times(1, 1))
                pool.tensor_copy(rows[:, bass.ds(b.times(1), 1), 0:D], xs[b.base % 2][:].unsqueeze(1)
                                 ).then_inc(s["xs_kept"], 1)

            def deviation(b):
                if not live(b):
                    return
                pool.wait_ge(s["mv_done"], b.times(1, 1))
                settle(pool)
                pool.tensor_scalar(vare[:], mv[:, 1:2], EPS, None, ALU.add).then_inc(s["vare_done"], 1)
                pool.wait_ge(s["vare_done"], b.times(1, 1))
                need(pool, s["xs_done"], b.times(1))
                pool.tensor_tensor(rstd[:], vare[:], mhalf[:, 0:1], ALU.pow).then_inc(s["rstd_done"], 1)

            def keep_top(b):
                if not live(b):
                    return
                pool.wait_ge(s["idx_done"], b.times(1, 1))
                col = bass.ds(b.times(1), 1)
                pool.tensor_copy(tv[:, :, col], top8[:, 0:TOP_K].unsqueeze(2)).then_inc(s["top_kept"], 1)
                pool.tensor_copy(ti[:, :, col], idx8[:, 0:TOP_K].unsqueeze(2)).then_inc(s["top_kept"], 1)

            def slots_of_group(q, i):
                cols = bass.ds(q.times(4), G)
                pool.wait_ge(s["rkg_done"], q.times(1, 1))
                pool.tensor_tensor(rkm[:], rkg[:], ohg[:], ALU.mult).then_inc(s["rkm_done"], 1)
                pool.wait_ge(s["rkm_done"], q.times(1, 1))
                pool.tensor_tensor(rkm[:, :, 0:4], rkm[:, :, 0:4], rkm[:, :, 4:8], ALU.add).then_inc(s["rankg_done"], 1)
                pool.wait_ge(s["rankg_done"], q.times(3, 1))
                pool.tensor_tensor(rkm[:, :, 0:2], rkm[:, :, 0:2], rkm[:, :, 2:4], ALU.add).then_inc(s["rankg_done"], 1)
                pool.wait_ge(s["rankg_done"], q.times(3, 2))
                pool.tensor_tensor(rankg[:].unsqueeze(2), rkm[:, :, 0:1], rkm[:, :, 1:2], ALU.add
                                   ).then_inc(s["rankg_done"], 1)
                pool.wait_ge(s["rankg_done"], q.times(3, 3))
                settle(pool)
                pool.tensor_scalar(skip[:], rankg[:], float(CAP), None, ALU.is_ge).then_inc(s["skipg"], 1)
                pool.wait_ge(s["skipg"], q.times(3, 1))
                pool.tensor_tensor(valid[:, 0, cols], one_g[:], skip[:], ALU.subtract).then_inc(s["skipg"], 1)
                pool.tensor_tensor(slotg[:], ti[:, 0, cols], cap_g[:], ALU.mult).then_inc(s["slotg_done"], 1)
                pool.wait_ge(s["slotg_done"], q.times(4, 1))
                pool.tensor_tensor(slotg[:], slotg[:], rankg[:], ALU.add).then_inc(s["slotg_done"], 1)
                pool.wait_ge(s["skipg"], q.times(3, 2))
                settle(pool)
                pool.tensor_scalar(skip[:], skip[:], float(FAR), None, ALU.mult).then_inc(s["skipg"], 1)
                pool.wait_ge(s["skipg"], q.times(3, 3))
                pool.wait_ge(s["slotg_done"], q.times(4, 2))
                pool.tensor_tensor(slotg[:], slotg[:], skip[:], ALU.add).then_inc(s["slotg_done"], 1)
                pool.wait_ge(s["slotg_done"], q.times(4, 3))
                need(pool, s["sc1"], q.times(64))
                settle(pool)
                pool.tensor_copy(slotig[i][:], slotg[:]).then_inc(s["slotg_done"], 1)
                pool.wait_ge(s["xs_kept"], q.times(4, 4))
                need(pool, s["sc1"], q.times(64))
                pool.tensor_copy(stage[:], rows[:, cols, :]).then_inc(s["staged"], 1)

            def scatter_group(q, i):
                pool.wait_ge(s["staged"], q.times(1, 1))
                pool.wait_ge(s["slotg_done"], q.times(4, 4))
                settle(pool)
                for t in range(G):
                    pool.indirect_dma_start(slots_d, bass.IndirectOffsetOnAxis(ap=slotig[i][:, t:t + 1], axis=0),
                                            stage[:, t, :], None, bounds_check=E * CAP - 1, oob_is_err=False
                                            ).then_inc(s["sc1"], 16)

            def step(j, u, r):
                g, q = group_of(r), ranked(r)
                v_beside_ones(j + 1)
                if u == 1 and g is not None:
                    add_bias(g)
                if u == 2 and g is not None:
                    third_k(g)
                if u == 3 and g is not None:
                    third_q(g)
                    if not (g.known and g.base >= NG - 1):
                        deviations(g + 1)
                if u == 0 and ranked(r + (-1)) is not None:
                    scatter_group(ranked(r + (-1)), 0)
                if u == 3 and q is not None:
                    slots_of_group(q, 0)
                keep_normed(j + (-2))
                deviation(j + (-1))
                keep_top(j + (-2))

            steps(pool, step, (3, 12, 64, 16 * NT))

            scatter_group(At(NG - 1, mult=1), 0)
            pool.wait_ge(s["staged"], NG)
            pool.tensor_copy(rows[:, :, D:D + 1].bitcast(I32), ids[:, 1, :].unsqueeze(2)).then_inc(s["rows2"], 1)
            pool.wait_ge(s["rows2"], 1)
            pool.wait_ge(s["rt2"], 13)
            for b in range(B):
                pool.indirect_dma_start(slots_d, bass.IndirectOffsetOnAxis(ap=sloti[:, b:b + 1], axis=0),
                                        rows[:, b, :], None, bounds_check=E * CAP - 1, oob_is_err=False
                                        ).then_inc(s["sc2"], 16)
            pool.wait_ge(s["rfills"], 16 * NG)

            def scatters(of):
                for u in range(2 * NCH):
                    pool.wait_ge(s["y_out"], of(2 * NCH, u + 1))
                    settle(pool)
                    for t in range(2):
                        pool.indirect_dma_start(result_d, bass.IndirectOffsetOnAxis(
                                                    ap=br[u % NCH][:, t, D:D + 1].bitcast(I32), axis=0),
                                                ys[u % NCH][:, t, :], None, bounds_check=TOP_K * N - 1,
                                                oob_is_err=False).then_inc(put[u % NCH], 16)

            pairs(pool, scatters)

        @block.scalar
        def _(act):
            act.wait_ge(s["bcol_ps"], 2)
            act.wait_ge(s["wgT_ps"], 1)
            act.copy(bq_col[:], bank[7][:, 0:1]).then_inc(s["bcol"], 1)
            act.copy(bk_col[:], bank[7][:, 1:2]).then_inc(s["bcol"], 1)
            act.copy(wgT[:], bank[7][:, 8:8 + E]).then_inc(s["bcol"], 1)
            act.wait_ge(s["bcol"], 3)

            def ctx_turned(g):
                act.wait_ge(s["cT_ps"], g.times(1, 1))
                need(act, s["v_ps"], g.times(1))
                act.copy(cTA[:], bank[6][:]).then_inc(s["cT_out"], 1)

            def first_k(g):
                act.wait_ge(s["k_ps"], g.times(1, 1))
                need(act, s["k3"], g.times(1))
                act.activation(kf[:], bank[6][:], ACT.Identity, bias=bk_col[:]).then_inc(s["kf_done"], 1)
                need(act, s["k_put"], g.times(16 * NT))
                act.activation(kp[:, 0, :], bank[6][:], ACT.Identity, bias=bk_col[:]).then_inc(s["k1"], 1)

            def second_k(g):
                act.wait_ge(s["kr_done"], g.times(1, 1))
                act.copy(kp[:, 1, :], kr[:]).then_inc(s["k2"], 1)

            def x_turned(g):
                act.wait_ge(s["xT_ps"], g.times(1, 1))
                need(act, s["q_ps"], g.times(1))
                act.copy(xTA[:], bank[6][:]).then_inc(s["xT_out"], 1)

            def first_q(g):
                act.wait_ge(s["q_ps"], g.times(1, 1))
                need(act, s["q3"], g.times(1))
                act.activation(qf[:], bank[6][:], ACT.Identity, bias=bq_col[:]).then_inc(s["qf_done"], 1)
                need(act, s["q_put"], g.times(16 * NT))
                act.activation(qp[:, 0, :], bank[6][:], ACT.Identity, bias=bq_col[:]).then_inc(s["q1"], 1)

            def second_q(g):
                act.wait_ge(s["qr_done"], g.times(1, 1))
                act.copy(qp[:, 1, :], qr[:]).then_inc(s["q2"], 1)

            for g in (At(0, mult=1), At(1, mult=1)):
                for part in (ctx_turned, first_k, x_turned, second_k, first_q, second_q):
                    part(g)

            def exps(b, c):
                if not live(b):
                    return
                act.wait_ge(s["s2"], b.times(4, c + 1))
                need(act, s["av"], b.times(4, c - 3))
                act.activation(pr[c][:], bank[2 + c % 2][:], ACT.Exp, scale=SCALE).then_inc(s["ex"], 1)

            def maxima_out(b):
                if not live(b):
                    return
                act.wait_ge(s["nT_ps"], b.times(1, 1))
                i = b.base % 4
                need(act, m_put[i], b.rounds16(-16))
                act.copy(nT[i][:], bank[7][0:3 * H, 0:S // 2].bitcast(BF16)).then_inc(s["nT_out"], 1)
                act.wait_ge(s["nT_out"], b.times(1, 1))
                act.dma_start(negmax_d[bass.ds(b.times(1), 1)].rearrange("o t (h q) -> (o t h) q", h=H), nT[i][:]
                              ).then_inc(m_put[i], 16)

            def keep_residual(b):
                if not live(b):
                    return
                act.wait_ge(s["x1_done"], b.times(1, 1))
                act.copy(xr[:, bass.ds(b.times(1), 1), :], x1[b.base % 2][:].unsqueeze(1)).then_inc(s["x1_kept"], 1)

            def normed_out(b):
                if not live(b):
                    return
                act.wait_ge(s["xsT_ps"], b.times(1, 1))
                need(act, s["lg"], b.times(1))
                act.copy(xsT[:], bank[7][:, 128:256]).then_inc(s["xsT_out"], 1)

            def context_out(b):
                if not live(b):
                    return
                act.wait_ge(s["cnT_ps"], b.times(1, 1))
                need(act, s["wo_ps"], b.times(1))
                act.copy(cnT[:], bank[5][:, 0:128]).then_inc(s["cnT_out"], 1)

            def weighted_out(b):
                if not live(b):
                    return
                act.wait_ge(s["av"], b.times(4, 4))
                need(act, s["nat"], b.times(1))
                act.copy(avs[:], bank[4][:]).then_inc(s["av_out"], 1)

            def step(j, u, r):
                g = group_of(r)
                maxima_out(j + 1)
                exps(j, 0)
                if u == 1 and g is not None:
                    first_k(g)
                if u == 2 and g is not None:
                    x_turned(g)
                if u == 3 and g is not None:
                    second_q(g)
                keep_residual(j + (-2))
                exps(j, 1)
                normed_out(j + (-2))
                exps(j, 2)
                context_out(j + (-1))
                if u == 0 and g is not None:
                    ctx_turned(g)
                if u == 2 and g is not None:
                    first_q(g)
                exps(j, 3)
                if u == 1 and g is not None:
                    second_k(g)
                weighted_out(j)

            steps(act, step, (16 * NT,))

            act.wait_ge(s["rt2"], 1)
            act.activation(pe2[:], pdiff[:], ACT.Exp).then_inc(s["pe_done"], 1)

            def hidden(of):
                for u in range(2 * NCH):
                    i = u % 2
                    act.wait_ge(s["bT_ps"], of(2 * NCH, u + 1))
                    need(act, s["h_ps"], of(2 * NCH, u - 1))
                    act.copy(bT[i][:], bank[i][:, 0:CH]).then_inc(s["bT_out"], 1)
                    act.wait_ge(s["h_ps"], of(2 * NCH, u + 1))
                    need(act, s["hs_done"], of(2 * NCH, u - 1))
                    for half in range(2):
                        act.activation(hr[i][:, 2 * half:2 * half + 2, :],
                                       bank[2 + 2 * i + half][:].rearrange("p (f c) -> p f c", f=2),
                                       ACT.Relu).then_inc(s["hr_done"], 1)

            pairs(act, hidden)

        @block.vector
        def _(dve):
            dve.memset(empty[:], 0.0).then_inc(s["empty0"], 1)
            dve.memset(zeros[:], 0.0).then_inc(s["zeroed"], 1)

            def clear(t):
                flat = t[:] if len(t[:].shape) == 2 else t[:].rearrange("p h w -> p (h w)")
                dve.memset(flat.bitcast(U32), 0).then_inc(s["zeroed"], 1)

            def row_x(g, t):
                return xr[:, bass.ds(g.times(4, t), 1), :].rearrange("p o d -> p (o d)")

            def statistics(g):
                dve.wait_ge(s[f"x_in{min(g.base, 2) if g.known else 2}"], 16)
                need(dve, s["mvA_done"], g.times(4))
                settle(dve)
                for t in range(G):
                    dve.bn_stats(stA[:, t, :], row_x(g, t)).then_inc(s["stA_done"], 1)

            def moments(g):
                need(dve, s["xnA_done"], g.times(4))
                dve.wait_ge(s["stA_done"], g.times(4, G))
                settle(dve)
                for t in range(G):
                    dve.bn_aggr(mvA[:, t, :], stA[:, t, :]).then_inc(s["mvA_done"], 1)

            def norm(g):
                dve.wait_ge(s["rstdA_done"], g.times(1, 1))
                need(dve, s["xT_ps"], g.times(1))
                for t in range(G):
                    dve.tensor_scalar(xnA[:, t, :], row_x(g, t), mvA[:, t, 0:1], rstdA[:, t:t + 1],
                                      ALU.subtract, ALU.mult).then_inc(s["xnA_done"], 1)

            def v_rows(g):
                dve.wait_ge(s["v_ps"], g.times(1, 1))
                dve.tensor_tensor(v_all[:, bass.ds(g.times(4), G), :],
                                  bank[6][:].rearrange("p (g d) -> p g d", g=G),
                                  bv_all[:].unsqueeze(1).to_broadcast([P, G, D]), ALU.add).then_inc(s["v_out"], 1)

            def rest_k(g):
                dve.wait_ge(s["kf_done"], g.times(1, 1))
                dve.wait_ge(s["k1"], g.times(1, 1))
                need(dve, s["k3"], g.times(1))
                dve.tensor_tensor(kr[:], kf[:], kp[:, 0, :], ALU.subtract).then_inc(s["kr_done"], 1)

            def rest_q(g):
                dve.wait_ge(s["qf_done"], g.times(1, 1))
                dve.wait_ge(s["q1"], g.times(1, 1))
                need(dve, s["q3"], g.times(1))
                dve.tensor_tensor(qr[:], qf[:], qp[:, 0, :], ALU.subtract).then_inc(s["qr_done"], 1)

            dve.wait_ge(s["b_in"], 64)
            for g in (At(0, mult=1), At(1, mult=1)):
                if g.base == 0:
                    statistics(g)
                    moments(g)
                norm(g)
                statistics(g + 1)
                moments(g + 1)
                rest_k(g)
                v_rows(g)
                for t in (qs, ks, km):
                    clear(t[2 * g.base])
                    clear(t[2 * g.base + 1])
                rest_q(g)
            for t in va:
                clear(t)
            dve.wait_ge(s["zeroed"], 15)
            for t in va:
                dve.memset(t[:, :, DH:DH + 1], 1.0).then_inc(s["zeroed"], 1)

            def maxes(b, c):
                if not live(b):
                    return
                dve.wait_ge(s["s1"], b.times(4, c + 1))
                if c == 0:
                    need(dve, s["n3"], b.times(1))
                dve.tensor_reduce(mxt[:, HC * c:HC * c + HC],
                                  bank[c % 2][:].rearrange("p (h k) -> p h k", h=HC), AX.X, ALU.max
                                  ).then_inc(s["mx"], 1)

            nat = bank[5][:].rearrange("p (h w) -> p h w", h=H)

            def sums(b):
                if not live(b):
                    return
                dve.wait_ge(s["nat"], b.times(1, 1))
                need(dve, s["cn_done"], b.times(1))
                dve.reciprocal(rden[:].unsqueeze(2), nat[:, :, DH:DH + 1]).then_inc(s["rec"], 1)

            def normal_context(b):
                if not live(b):
                    return
                need(dve, s["cnT_ps"], b.times(1))
                dve.wait_ge(s["rec"], b.times(1, 1))
                dve.tensor_tensor(cn[:].rearrange("p (h d) -> p h d", h=H), nat[:, :, 0:DH],
                                  rden[:].unsqueeze(2).to_broadcast([P, H, DH]), ALU.mult
                                  ).then_inc(s["cn_done"], 1)

            logits = bank[7][:, 256:256 + E]

            def top_values(b):
                if not live(b):
                    return
                dve.wait_ge(s["lg"], b.times(1, 1))
                need(dve, s["top_kept"], _twice(dve, b))
                settle(dve)
                dve.max(out=top8[:], in_=logits).then_inc(s["top_done"], 1)

            def top_experts(b):
                if not live(b):
                    return
                dve.wait_ge(s["top_done"], b.times(1, 1))
                settle(dve)
                dve.max_index(out=idx8[:], in_max=top8[:], in_values=logits).then_inc(s["idx_done"], 1)

            def residual(b):
                if not live(b):
                    return
                i = b.base % 2
                dve.wait_ge(s["wo_ps"], b.times(1, 1))
                need(dve, s["x1_kept"], b.times(1, -1))
                need(dve, s["xs_done"], b.times(1, -1))
                if b.known and b.base == 0:
                    dve.wait_ge(s["xbo"], 1)
                dve.tensor_tensor(x1[i][:].unsqueeze(1), bank[5][:, 128:256].unsqueeze(1),
                                  xr[:, bass.ds(b.times(1), 1), :], ALU.add).then_inc(s["x1_done"], 1)

            def residual_statistics(b):
                if not live(b):
                    return
                dve.wait_ge(s["x1_done"], b.times(1, 1))
                need(dve, s["mv_done"], b.times(1))
                dve.bn_stats(st[:], x1[b.base % 2][:]).then_inc(s["st_done"], 1)

            def residual_moments(b):
                if not live(b):
                    return
                dve.wait_ge(s["st_done"], b.times(1, 1))
                need(dve, s["xs_done"], b.times(1))
                settle(dve)
                dve.bn_aggr(mv[:], st[:]).then_inc(s["mv_done"], 1)

            def negative_max(b, part):
                if not live(b):
                    return
                if part == 0:
                    need(dve, s["nT_ps"], b.times(1))
                    dve.wait_ge(s["mx"], b.times(4, 4))
                    dve.tensor_scalar(nparts[:, 0, :], mxt[:], -1.0, None, ALU.mult).then_inc(s["n1"], 1)
                if part == 1:
                    dve.wait_ge(s["n1"], b.times(1, 1))
                    dve.scalar_tensor_tensor(out=nrem[:], in0=mxt[:], scalar=-1.0, in1=nparts[:, 0, :],
                                             op0=ALU.mult, op1=ALU.subtract).then_inc(s["nr"], 1)
                if part == 2:
                    dve.wait_ge(s["nr"], b.times(1, 1))
                    dve.tensor_copy(nparts[:, 1, :], nrem[:]).then_inc(s["n2"], 1)
                if part == 3:
                    dve.wait_ge(s["n2"], b.times(1, 1))
                    dve.tensor_tensor(nparts[:, 2, :], nrem[:], nparts[:, 1, :], ALU.subtract).then_inc(s["n3"], 1)

            def normed(b):
                if not live(b):
                    return
                i = b.base % 2
                dve.wait_ge(s["rstd_done"], b.times(1, 1))
                need(dve, s["xsT_ps"], b.times(1, -1))
                need(dve, s["xs_kept"], b.times(1, -1))
                dve.tensor_scalar(xs[i][:], x1[i][:], mv[:, 0:1], rstd[:], ALU.subtract, ALU.mult
                                  ).then_inc(s["xs_done"], 1)

            def one_hot_group(q):
                dve.wait_ge(s["top_kept"], q.times(8, 8))
                need(dve, s["rkm_done"], q.times(1))
                if q.known and q.base == 0:
                    dve.wait_ge(s["c_ready"], 2)
                dve.tensor_tensor(ohg[:], ti[:, 0, bass.ds(q.times(4), G)].unsqueeze(2).to_broadcast([P, G, E]),
                                  ioE[:].unsqueeze(1).to_broadcast([P, G, E]), ALU.is_equal
                                  ).then_inc(s["ohg_done"], 1)

            gr = bank[6][:, 0:(G + 1) * E].rearrange("p (t e) -> p t e", e=E)

            def rank_group(q):
                dve.wait_ge(s["rkg_ps"], q.times(1, 1))
                need(dve, s["carried"], q.times(1))
                need(dve, s["rkm_done"], q.times(1))
                dve.tensor_tensor(rkg[:], gr[:, 0:G, :], carry[:].unsqueeze(1).to_broadcast([P, G, E]), ALU.add
                                  ).then_inc(s["rkg_done"], 1)

            def carry_group(q):
                dve.wait_ge(s["rkg_done"], q.times(1, 1))
                dve.tensor_tensor(carry[:].unsqueeze(1), carry[:].unsqueeze(1), gr[:, G:G + 1, :], ALU.add
                                  ).then_inc(s["carried"], 1)

            def step(j, u, r):
                g, q = group_of(r), ranked(r)
                ahead, last, second = j + 2, j + (-1), j + (-2)
                maxes(ahead, 0)
                if u == 3 and q is not None:
                    rank_group(q)
                normed(second)
                sums(last)
                maxes(ahead, 1)
                normal_context(last)
                if u == 2 and q is not None:
                    one_hot_group(q)
                if u == 3 and q is not None:
                    carry_group(q)
                if u == 0 and g is not None:
                    norm(g)
                if u == 1 and g is not None:
                    rest_k(g)
                if u == 2 and g is not None and not (g.known and g.base >= NG - 1):
                    statistics(g + 1)
                if u == 3 and g is not None and not (g.known and g.base >= NG - 1):
                    moments(g + 1)
                maxes(ahead, 2)
                if u == 1 and g is not None:
                    v_rows(g)
                if u == 2 and g is not None:
                    rest_q(g)
                maxes(ahead, 3)
                negative_max(ahead, 0)
                residual(last)
                negative_max(ahead, 1)
                residual_statistics(last)
                negative_max(ahead, 2)
                residual_moments(last)
                top_values(second)
                negative_max(ahead, 3)
                top_experts(second)

            steps(dve, step, (3, 8))

            n = [0]

            def link(ins):
                n[0] += 1
                ins.then_inc(s["rt2"], 1)
                dve.wait_ge(s["rt2"], n[0])

            dve.wait_ge(s["top_kept"], 2 * B)
            dve.wait_ge(s["carried"], NG)
            link(dve.tensor_tensor(pdiff[:], tv[:, 1, :], tv[:, 0, :], ALU.subtract))
            link(dve.tensor_tensor(oh[:], ti[:, 1, :].unsqueeze(2).to_broadcast([P, B, E]),
                                   ioE[:].unsqueeze(1).to_broadcast([P, B, E]), ALU.is_equal))
            dve.wait_ge(s["cnt_ps"], 1)
            link(dve.tensor_copy(cnt[:], bank[1][:, 0:B * E].rearrange("p (t e) -> p e t", e=E)))
            link(dve.tensor_tensor_scan(cum[:].rearrange("p e t -> p (e t)"), seg[:].rearrange("p e t -> p (e t)"),
                                        cnt[:].rearrange("p e t -> p (e t)"), 0.0, ALU.mult, ALU.add))
            link(dve.tensor_tensor(cum[:], cum[:], cnt[:], ALU.subtract))
            link(dve.tensor_tensor(rk[:], bank[0][:, 0:B * E].rearrange("p (t e) -> p t e", e=E),
                                   cum[:].rearrange("p e t -> p t e"), ALU.add))
            link(dve.tensor_tensor(rk[:], rk[:], carry[:].unsqueeze(1).to_broadcast([P, B, E]), ALU.add))
            link(dve.tensor_tensor(rk[:], rk[:], oh[:], ALU.mult))
            link(dve.tensor_reduce(rank[:], rk[:], AX.X, ALU.add))
            dve.tensor_scalar(valid[:, 1, :], rank[:], float(CAP), None, ALU.is_lt).then_inc(s["rt2"], 1)
            dve.scalar_tensor_tensor(out=slot[:], in0=ti[:, 1, :], scalar=float(CAP), in1=rank[:],
                                     op0=ALU.mult, op1=ALU.add).then_inc(s["rt2"], 1)
            n[0] += 2
            dve.wait_ge(s["rt2"], n[0])
            link(dve.scalar_tensor_tensor(out=rank[:], in0=valid[:, 1, :], scalar=float(-FAR), in1=slot[:],
                                          op0=ALU.mult, op1=ALU.add))
            link(dve.tensor_scalar(sloti[:], rank[:], float(FAR), None, ALU.add))
            dve.wait_ge(s["pe_done"], 1)
            link(dve.tensor_scalar(psumr[:], pe2[:], 1.0, None, ALU.add))
            link(dve.reciprocal(pdiff[:], psumr[:]))
            dve.wait_ge(s["skipg"], 3 * NG)
            link(dve.tensor_tensor(prob[:, 0, :], pdiff[:], valid[:, 0, :], ALU.mult))
            link(dve.tensor_tensor(pe2[:], pe2[:], pdiff[:], ALU.mult))
            link(dve.tensor_tensor(prob[:, 1, :], pe2[:], valid[:, 1, :], ALU.mult))
            dve.wait_ge(s["x1_kept"], B)

            def squares(of):
                def result_rows(u):
                    dve.wait_ge(s["y_ps"], of(2 * NCH, u + 1))
                    need(dve, put[u % NCH], of(64, 32 * (u // NCH)))
                    dve.tensor_copy(ys[u % NCH][:], bank[6 + u % 2][:, 0:CH].rearrange("p (t d) -> p t d", t=2)
                                    ).then_inc(s["y_out"], 1)

                for u in range(2 * NCH):
                    i = u % 2
                    dve.wait_ge(s["hr_done"], of(4 * NCH, 2 * u + 2))
                    need(dve, s["y_ps"], of(2 * NCH, u - 1))
                    dve.tensor_tensor(hs[i], hr[i], hr[i], ALU.mult).then_inc(s["hs_done"], 1)
                    if u:
                        result_rows(u - 1)
                result_rows(2 * NCH - 1)

            pairs(dve, squares)

            for g in range(NG):
                y = ya[g % 2]
                dve.wait_ge(s[f"ya_in{g % 2}"], 32 * (g // 2 + 1))
                for t in range(G):
                    b = G * g + t
                    dve.scalar_tensor_tensor(out=xr[:, b, :], in0=y[0][:, t, :], scalar=prob[:, 0, b:b + 1],
                                             in1=xr[:, b, :], op0=ALU.mult, op1=ALU.add).then_inc(s["e1"], 1)
                for t in range(G):
                    b = G * g + t
                    dve.wait_ge(s["e1"], b + 1)
                    dve.scalar_tensor_tensor(out=xr[:, b, :], in0=y[1][:, t, :], scalar=prob[:, 1, b:b + 1],
                                             in1=xr[:, b, :], op0=ALU.mult, op1=ALU.add).then_inc(s["e2"], 1)

        @block.tensor
        def _(pe):
            pe.wait_ge(s["wperm"], 4)
            pe.wait_ge(s["rt"], 3)
            for i in range(2):
                pe.matmul(bank[7][:, i:i + 1], bqk_row[0:1, i, :], ident[0:1, 0:1], start=True, stop=True
                          ).then_inc(s["bcol_ps"], 1)
            pe.wait_ge(s["g_in"], 16)
            pe.transpose(bank[7][:, 8:8 + E], wg_raw[:], ident[0:E, 0:E]).then_inc(s["wgT_ps"], 1)

            def turn_ctx(g):
                pe.wait_ge(s["c_inn"], g.times(16, 16))
                need(pe, s["q1"], g.times(1))
                if not g.known or g.base > 2:
                    pe.wait_ge(s["carried"], g.times(1, -3))
                for t in range(G):
                    mm = pe.transpose(bank[6][:, t * S:(t + 1) * S], c_in[:, t, :], ident[:])
                mm.then_inc(s["cT_ps"], 1)

            def project_k(g):
                pe.wait_ge(s["cT_out"], g.times(1, 1))
                pe.matmul(bank[6][:], wk_s[:], cTA[:], start=True, stop=True).then_inc(s["k_ps"], 1)

            def project_v(g):
                pe.wait_ge(s["k1"], g.times(1, 1))
                for t in range(G):
                    mm = pe.matmul(bank[6][:, t * D:(t + 1) * D], cTA[:, t * S:(t + 1) * S], wv_s[:],
                                   start=True, stop=True)
                mm.then_inc(s["v_ps"], 1)

            def turn_x(g):
                pe.wait_ge(s["xnA_done"], g.times(4, G))
                pe.wait_ge(s["v_out"], g.times(1, 1))
                for t in range(G):
                    mm = pe.transpose(bank[6][:, t * S:(t + 1) * S], xnA[:, t, :], ident[:])
                mm.then_inc(s["xT_ps"], 1)

            def project_q(g):
                pe.wait_ge(s["xT_out"], g.times(1, 1))
                pe.matmul(bank[6][:], wq_s[:], xTA[:], start=True, stop=True).then_inc(s["q_ps"], 1)

            for g in (At(0, mult=1), At(1, mult=1)):
                for part in (turn_ctx, project_k, project_v, turn_x, project_q):
                    part(g)
            pe.wait_ge(s["bcol"], 3)

            def scores_for_max(b, c):
                i = b.base % 4
                if c == 0:
                    pe.wait_ge(q_in[i], b.rounds16())
                    pe.wait_ge(km_in[i], b.rounds16())
                need(pe, s["mx"], b.times(4, c - 1))
                for h in range(HC):
                    cols = slice((HC * c + h) * S, (HC * c + h + 1) * S)
                    mm = pe.matmul(bank[c % 2][:, h * S:(h + 1) * S], qs[i][:, cols], km[i][:, cols],
                                   start=True, stop=True)
                mm.then_inc(s["s1"], 1)

            def scores_for_exp(b, c):
                i = b.base % 4
                if c == 0:
                    pe.wait_ge(k_in[i], b.rounds16(16))
                    pe.wait_ge(m_in[i], b.rounds16())
                need(pe, s["ex"], b.times(4, c - 1))
                for h in range(HC):
                    cols = slice((HC * c + h) * S, (HC * c + h + 1) * S)
                    mm = pe.matmul(bank[2 + c % 2][:, h * S:(h + 1) * S], ks[i][:, cols], qs[i][:, cols],
                                   start=True, stop=True)
                mm.then_inc(s["s2"], 1)

            def times_v(b, c):
                pe.wait_ge(s["ex"], b.times(4, c + 1))
                if c == 0:
                    pe.wait_ge(s["va_in"], b.times(1, 1))
                    need(pe, s["av_out"], b.times(1))
                for h in range(HC):
                    mm = pe.matmul(bank[4][VW * h:VW * (h + 1), c * S:(c + 1) * S],
                                   va[b.base % 2][:, HC * c + h, :], pr[c][:, h * S:(h + 1) * S],
                                   start=True, stop=True, tile_position=(0, VW * h))
                mm.then_inc(s["av"], 1)

            def context_back(b):
                pe.wait_ge(s["av_out"], b.times(1, 1))
                need(pe, s["x1_done"], b.times(1))
                for c in range(NC):
                    mm = pe.transpose(bank[5][:, c * S:(c + 1) * S], avs[:, c * S:(c + 1) * S], ident[:])
                mm.then_inc(s["nat"], 1)

            def context_turned(b):
                pe.wait_ge(s["cn_done"], b.times(1, 1))
                pe.transpose(bank[5][:, 0:128], cn[:], ident[:]).then_inc(s["cnT_ps"], 1)

            def output_rows(b):
                pe.wait_ge(s["cnT_out"], b.times(1, 1))
                pe.matmul(bank[5][:, 128:256], cnT[:], wo_s[:], start=True, stop=True).then_inc(s["wo_ps"], 1)

            def maxima_turned(b):
                pe.wait_ge(s["n3"], b.times(1, 1))
                if b.known and b.base < 4:
                    need(pe, s["nT_out"], b.base)
                need(pe, s["idx_done"], b.times(1, -3))
                pe.transpose(bank[7][:, 0:S // 2].bitcast(BF16), nparts_pad[:], identb[:]).then_inc(s["nT_ps"], 1)

            def normed_turned(b):
                pe.wait_ge(s["xs_done"], b.times(1, 1))
                pe.wait_ge(s["nT_out"], min(b.base + 4, B) if b.known else b.times(1, 4))
                need(pe, s["idx_done"], b.times(1))
                pe.transpose(bank[7][:, 128:256], xs[b.base % 2][:], ident[:]).then_inc(s["xsT_ps"], 1)

            def logits(b):
                pe.wait_ge(s["xsT_out"], b.times(1, 1))
                pe.matmul(bank[7][:, 256:256 + E], xsT[:], wgT[:], start=True, stop=True).then_inc(s["lg"], 1)

            def count_group(q):
                pe.wait_ge(s["ohg_done"], q.times(1, 1))
                pe.wait_ge(s["q1"], min(q.base + 4, NG) if q.known else q.times(1, 4))
                need(pe, s["carried"], q.times(1))
                ohf = ohg[:].rearrange("p t e -> p (t e)")
                pe.matmul(bank[6][:, 0:G * E], before[:], ohf, start=True, stop=False, skip_group_check=True)
                for t in range(G):
                    mm = pe.matmul(bank[6][:, (t + 1) * E:(G + 1) * E].rearrange("p (n e) -> p n e", e=E), onesb[:],
                                   ohg[:, t:t + 1, :].to_broadcast([P, G - t, E]),
                                   start=False, stop=(t == G - 1), skip_group_check=True)
                mm.then_inc(s["rkg_ps"], 1)

            def step(j, u, r):
                g, q = group_of(r), ranked(r)
                ahead, now, last, second = j + 2, j, j + (-1), j + (-2)
                for c in range(NC):
                    if live(ahead):
                        scores_for_max(ahead, c)
                    if c == 0 and live(j + 1):
                        maxima_turned(j + 1)
                    if live(now):
                        scores_for_exp(now, c)
                        if c:
                            times_v(now, c - 1)
                    if c == 0 and live(last):
                        context_back(last)
                    if c == 1 and live(second):
                        normed_turned(second)
                    if c == 2 and live(second):
                        logits(second)
                    if c == 2 and live(last):
                        context_turned(last)
                    if c == 3 and live(last):
                        output_rows(last)
                    if g is not None:
                        if (u, c) == (0, 1):
                            turn_ctx(g)
                        if (u, c) == (0, 3):
                            project_k(g)
                        if (u, c) == (1, 1):
                            project_v(g)
                        if (u, c) == (1, 3):
                            turn_x(g)
                        if (u, c) == (2, 1):
                            project_q(g)
                    if (u, c) == (2, 3) and q is not None:
                        count_group(q)
                if live(now):
                    times_v(now, NC - 1)

            steps(pe, step, ())

            pe.wait_ge(s["rt2"], 2)
            ohf = oh[:].rearrange("p t e -> p (t e)")
            pe.matmul(bank[0][:, 0:B * E], before[:], ohf, start=True, stop=True)
            pe.matmul(bank[1][:, 0:B * E], onesb[:], ohf, start=True, stop=True).then_inc(s["cnt_ps"], 1)
            pe.wait_ge(s["rt2"], 6)

            def chunks(of):
                def turn(u):
                    i = u % 2
                    pe.wait_ge(br_in[u % NCH], of(32, 16 * (u // NCH + 1)))
                    need(pe, s["bT_out"], of(2 * NCH, u - 1))
                    for t in range(2):
                        mm = pe.transpose(bank[i][:, t * P:(t + 1) * P], br[u % NCH][:, t, 0:D], ident[:])
                    mm.then_inc(s["bT_ps"], 1)

                def up(u):
                    i = u % 2
                    w = w1[u // NCH]
                    if u % NCH == 0:
                        pe.wait_ge(s[f"w_in{u // NCH}"], of(32, 32))
                    pe.wait_ge(s["bT_out"], of(2 * NCH, u + 1))
                    need(pe, s["hr_done"], of(4 * NCH, 2 * u - 2))
                    for f in range(NF):
                        mm = pe.matmul(bank[2 + 2 * i + f // 2][:, (f % 2) * CH:(f % 2 + 1) * CH],
                                       w[:, f * P:(f + 1) * P], bT[i][:], start=True, stop=True)
                    mm.then_inc(s["h_ps"], 1)

                def down(u):
                    i = u % 2
                    w = w2[u // NCH]
                    pe.wait_ge(s["hs_done"], of(2 * NCH, u + 1))
                    need(pe, s["y_out"], of(2 * NCH, u - 1))
                    for t in range(2):
                        for f in range(NF):
                            mm = pe.matmul(bank[6 + i][:, t * D:(t + 1) * D], hs[i][:, f, t * P:(t + 1) * P],
                                           w[:, f, :], start=(f == 0), stop=(f == NF - 1))
                    mm.then_inc(s["y_ps"], 1)

                turn(0)
                for u in range(2 * NCH):
                    if u + 1 < 2 * NCH:
                        turn(u + 1)
                    up(u)
                    if u:
                        down(u - 1)
                down(2 * NCH - 1)

            pairs(pe, chunks)


_INS = ['x', 'ctx_1024', 'L0_xattn_Wq', 'L0_xattn_bq', 'L0_xattn_Wk', 'L0_xattn_bk', 'L0_xattn_Wv', 'L0_xattn_bv',
        'L0_xattn_Wo', 'L0_xattn_bo', 'L0_ffn_w_g', 'L0_ffn_c_fc', 'L0_ffn_c_proj']
_OUT = ((32, 128, 128), 'float32')


def kernel(**inputs):
    import numpy as np
    import concourse.bacc as bacc
    from concourse.bass_utils import run_bass_kernel_spmd as run

    nc = bacc.Bacc("TRN2", target_bir_lowering=False, num_devices=1)
    arrays, args = {}, []
    for name in _INS:
        a = np.ascontiguousarray(inputs[name])
        arrays[f"in_{name}"] = a
        args.append(nc.dram_tensor(f"in_{name}", a.shape, mybir.dt.from_np(a.dtype), kind="ExternalInput").ap())
    shape, dtype = _OUT
    args.append(nc.dram_tensor("out_0", shape, mybir.dt.from_np(np.dtype(dtype)), kind="ExternalOutput").ap())
    xattn_moe_kernel(nc, *args)
    r = run(nc, [arrays], core_ids=[0])
    return r.results[0]["out_0"]
```

```python
from contextlib import ExitStack
from itertools import islice

import concourse.bass as bass
from concourse import mybir

ALU = mybir.AluOpType
ACT = mybir.ActivationFunctionType
AX = mybir.AxisListType
F32 = mybir.dt.float32
F32R = mybir.dt.float32r
BF16 = mybir.dt.bfloat16
I32 = mybir.dt.int32
U32 = mybir.dt.uint32

P = 128
Q_TERMS = (0, 0, 0, 1, 2, 1)
K_TERMS = (1, 2, 0, 0, 0, 1)
EPS = 1e-5
TOP_K = 2


class At:

    def __init__(self, base, regs=None, mult=4):
        self.base, self.regs, self.mult = base, regs, mult

    def times(self, k, plus=0):
        const = k * self.base + plus
        return const if self.regs is None else self.regs[k * self.mult] + const

    def rounds16(self, plus=0):
        const = 16 * (self.base // 4 + 1) + plus
        return const if self.regs is None else self.regs[16] + const

    def group(self):
        const = self.base // 4
        return const if self.regs is None else self.regs[1] + const

    def __add__(self, n):
        return At(self.base + n, self.regs, self.mult)

    @property
    def known(self):
        return self.regs is None


def xattn_moe_kernel(nc, x, ctx, Wq, bq, Wk, bk, Wv, bv, Wo, bo, w_g, c_fc, c_proj, out):
    B, S, D = x.shape
    E, _, F = c_fc.shape
    H = 16
    DH = D // H
    NF = F // P
    N = B * S
    CAP = int(1.25 * N * TOP_K / E)
    G = 4
    NG = B // G
    NT = len(Q_TERMS)
    KR = NT * DH
    KC = 96
    HC = 4
    NC = H // HC
    VW = 32
    RW = 132
    CH = 256
    NCH = CAP // CH
    SCALE = 1.0 / float(DH) ** 0.5
    STORED = 16 * 3
    SCATTERED = 16 * TOP_K * G
    FAR = 100000
    FILLS = 40
    STEP_FILLS = 3
    LO, HI = 3, NG - 3
    assert S == P and D == P and E == 8 and CAP % CH == 0 and B % 4 == 0

    def dram(name, shape, dt):
        return nc.dram_tensor(name, shape, dt, kind="Internal").ap()

    q_stack_d = dram("q_stack_d", (NG, NT, P, G * S), BF16)
    k_stack_d = dram("k_stack_d", (NG, NT, P, G * S), BF16)
    slots_d = dram("slots_d", (E * 2 * CAP, RW), F32)
    result_d = dram("result_d", (TOP_K * N, D), F32)

    with ExitStack() as es:
        def sb(name, shape, dt=F32):
            return es.enter_context(nc.sbuf_tensor(name, shape, dt))

        def sem(name):
            return es.enter_context(nc.semaphore(name))

        bank = [es.enter_context(nc.psum_tensor(f"bank{i}", [P, 512], F32)) for i in range(8)]

        ident = sb("ident", [P, P])
        identb = sb("identb", [P, P], BF16)
        before = sb("before", [P, P], BF16)
        onesb = sb("onesb", [P, P], BF16)
        ones_rows = sb("ones_rows", [3, H * S], BF16)
        ioE = sb("ioE", [P, E])
        ids = sb("ids", [P, TOP_K, B], I32)
        mhalf = sb("mhalf", [P, G])
        wq_raw = sb("wq_raw", [P, D])
        wk_raw = sb("wk_raw", [P, D])
        wq_s = sb("wq_s", [P, D])
        wk_s = sb("wk_s", [P, D])
        wv_s = sb("wv_s", [P, D])
        wo_s = sb("wo_s", [P, D])
        carry = sb("carry", [P, TOP_K * E])
        bq_col = sb("bq_col", [P, 1])
        bk_col = sb("bk_col", [P, 1])
        bv_all = sb("bv_all", [P, D])
        bo_all = sb("bo_all", [P, D])
        wg_raw = sb("wg_raw", [E, D])
        wgT = sb("wgT", [P, E])
        empty = sb("empty", [P, 4, RW])
        zeros = sb("zeros", [P, 4, D])

        xr = sb("xr", [P, B, D])
        c_in = sb("c_in", [P, G, D])
        v_all = sb("v_all", [P, B, D])
        stA = sb("stA", [P, G, 6])
        mvA = sb("mvA", [P, G, 2])
        vareA = sb("vareA", [P, G])
        rstdA = sb("rstdA", [P, G])
        xnA = sb("xnA", [P, G, D])
        xTA = sb("xTA", [P, G * S])
        cTA = sb("cTA", [P, G * S])
        qr = sb("qr", [P, G * S])
        kr = sb("kr", [P, G * S])
        qp = sb("qp", [P, 3, G * S], BF16)
        kp = sb("kp", [P, 3, G * S], BF16)

        qs = [sb(f"qs{i}", [KC, H * S], BF16) for i in range(4)]
        ks = [sb(f"ks{i}", [KC, H * S], BF16) for i in range(4)]
        km = [sb(f"km{i}", [KC, H * S], BF16) for i in range(4)]
        va = [sb(f"va{i}", [P, H, VW]) for i in range(2)]
        mxt = [sb(f"mxt{i}", [P, H]) for i in range(2)]
        nrem = sb("nrem", [P, H])
        nparts_pad = sb("nparts_pad", [P, P], BF16)
        nparts = nparts_pad[:, 0:3 * H].rearrange("p (t h) -> p t h", t=3)
        nT = [sb(f"nT{i}", [3 * H, S], BF16) for i in range(4)]
        pr = [sb(f"pr{i}", [P, HC * S]) for i in range(4)]
        avs = sb("avs", [P, NC * S])
        rden = sb("rden", [P, H])
        cn = sb("cn", [P, D])
        cnT = sb("cnT", [P, S])
        x1 = [sb(f"x1_{i}", [P, D]) for i in range(2)]
        st = sb("st", [P, 6])
        mv = sb("mv", [P, 2])
        vare = sb("vare", [P, 1])
        rstd = sb("rstd", [P, 1])
        xs = [sb(f"xs{i}", [P, D]) for i in range(2)]
        xsT = sb("xsT", [P, S])
        top8 = sb("top8", [P, E])
        idx8 = sb("idx8", [P, E], U32)
        rows = sb("rows", [P, B, D])

        tv = sb("tv", [P, TOP_K, B])
        ti = sb("ti", [P, TOP_K, B])
        ohg = sb("ohg", [P, G, TOP_K * E], BF16)
        rkg = sb("rkg", [P, G, TOP_K * E])
        rkm = sb("rkm", [P, G, TOP_K * E])
        rankg = sb("rankg", [P, G, TOP_K])
        skip = sb("skip", [P, G, TOP_K])
        slotg = sb("slotg", [P, G, TOP_K])
        away = sb("away", [P, G, TOP_K])
        slotig = sb("slotig", [P, G, TOP_K], I32)
        stage = sb("stage", [P, TOP_K, G, RW])
        cap_g = sb("cap_g", [P, G, TOP_K])
        turn_g = sb("turn_g", [P, G, TOP_K])
        mid_g = sb("mid_g", [P, G, TOP_K])
        window0 = sb("window0", [P, E])
        firsts = sb("firsts", [P, E])
        starts = sb("starts", [P, E], I32)
        ranks = sb("ranks", [P, TOP_K, B])
        oh = sb("oh", [P, B, E])
        rank = sb("rank", [P, B])
        valid = sb("valid", [P, TOP_K, B])
        pdiff = sb("pdiff", [P, B])
        pe2 = sb("pe2", [P, B])
        psumr = sb("psumr", [P, B])
        prob = sb("prob", [P, TOP_K, B])

        w1 = sb("w1", [P, F])
        w2 = sb("w2", [P, NF * D])
        w1h = [sb(f"w1h{i}", [P, F], F32R) for i in range(2)]
        w1l = [sb(f"w1l{i}", [P, F], F32R) for i in range(2)]
        w2h = [sb(f"w2h{i}", [P, NF * D], F32R) for i in range(2)]
        w2l = [sb(f"w2l{i}", [P, NF * D], F32R) for i in range(2)]
        bTh = [sb(f"bTh{i}", [P, CH], F32R) for i in range(2)]
        bTl = [sb(f"bTl{i}", [P, CH], F32R) for i in range(2)]
        hh = [sb(f"hh{i}", [P, NF * CH], F32R) for i in range(2)]
        hl = [sb(f"hl{i}", [P, NF * CH], F32R) for i in range(2)]
        room = v_all[:].rearrange("p b d -> p (b d)").rearrange("p (i c) -> p i c", i=4)
        hr = [room[:, i] for i in range(2)]
        sq = [room[:, 2 + i] for i in range(2)]
        SQ = (NF - 1) * CH
        room2 = rows[:].rearrange("p b d -> p (b d)")
        at = [0]

        def part_of_room2(n):
            at[0] += n
            assert at[0] <= B * D
            return room2[:, at[0] - n:at[0]]

        br = [part_of_room2(2 * RW).rearrange("p (t w) -> p t w", t=2) for _ in range(2 * NCH)]
        ys = [part_of_room2(2 * D).rearrange("p (t d) -> p t d", t=2) for _ in range(NCH)]
        yT = [sb(f"yT{i}", [P, CH]) for i in range(2)]

        YR = 4
        ya = v_all[:].rearrange("p (i k g) d -> p i k g d", i=YR, k=TOP_K)
        ya = [[ya[:, i, k] for k in range(TOP_K)] for i in range(YR)]

        names = """wk_in wq_in b_in g_in v_in o_in c_ready e_ready wperm wgT_ps wgT_out fills rfills
            zeroed zeroed3 empty0 x_in0 x_in1 x_in2 c_inn stA_done mvA_done vareA_done rstdA_done xnA_done
            xbo xT_ps cT_ps xT_out cT_out q_ps k_ps v_ps q1 k1 qr_done kr_done q2 k2 q3 k3 v_out q_put k_put
            s1 mx n1 nr n2 n3 nT_ps nT_out s2 ex av va_in av_out nat rec cn_done cnT_ps cnT_out wo_ps
            x1_done st_done mv_done vare_done rstd_done xs_done x1_kept xs_kept xsT_ps xsT_out lg top_done
            idx_done top_kept ohg_done rkg_ps rkg_done carried rkm_done rankg_done skipg slotg_done staged
            sc1 ids_staged starts_done prob_done rt rt2 pe_done w1_in w2_in w_high w_low bT_ps bT_high
            bT_low h_ps hr_done sq_done sq2_done hh_done hl_done y_ps yT_out back_ps y_out weighted added summed
            settled""".split()
        s = {n: sem(n) for n in names}
        q_in = [sem(f"q_in{i}") for i in range(4)]
        k_in = [sem(f"k_in{i}") for i in range(4)]
        km_in = [sem(f"km_in{i}") for i in range(4)]
        m_in = [sem(f"m_in{i}") for i in range(4)]
        br_in = [sem(f"br_in{i}") for i in range(2 * NCH)]
        ya_in = [sem(f"ya_in{i}") for i in range(YR)]
        out_put = [sem(f"out_put{i}") for i in range(YR)]
        put = [sem(f"put{i}") for i in range(NCH)]

        def need(eng, what, value):
            if not isinstance(value, int) or value > 0:
                eng.wait_ge(what, value)

        def settle(eng):
            eng.sem_inc(s["settled"], 1)

        def steps(eng, body, keys=()):
            for j in range(-2, LO * G):
                body(At(j), j % G, At(j // G, mult=1))
            with eng.Fori(LO, HI) as r:
                regs = {1: r, 4: eng.snap(r * 4), 16: eng.snap(r * 16)}
                for k in keys:
                    regs[k] = eng.snap(r * k)
                for u in range(G):
                    body(At(u, regs), u, At(0, regs, 1))
            for j in range(HI * G, B + 4):
                body(At(j), j % G, At(j // G, mult=1))

        def group_of(r):
            g = r + 2
            return g if not g.known or 2 <= g.base < NG else None

        def ranked(r):
            q = r + (-1)
            return q if not q.known or 0 <= q.base < NG else None

        def chunks(eng, body, lag=0):
            for u in range(2 * NCH):
                body(lambda k, plus: plus, u)
            with eng.Fori(1, E // 2) as pair:
                held = {k: eng.snap(pair * k) for k in (2, 4, 16, 32, 64, 2 * NCH, 4 * NCH)}
                for u in range(2 * NCH):
                    body(lambda k, plus: held[k] + plus, u)
            for u in range(lag):
                body(lambda k, plus: k * (E // 2) + plus, u)

        def there(of, v):
            c = of(2 * NCH, v)
            return not isinstance(c, int) or 0 <= c < E * NCH

        def live(b):
            return not b.known or 0 <= b.base < B

        def next_expert(eng, of, plus):
            e = of(2, plus)
            return e % E if isinstance(e, int) else eng.snap(e % E)

        def twice(b):
            return 2 * b.base if b.known else b.times(1) * 2

        block = es.enter_context(nc.Block())

        @block.sync
        def _(sp):
            xg = x.rearrange("b s d -> s b d")
            cg = ctx.rearrange("b s d -> s b d")

            def load_ctx(g):
                need(sp, s["cT_ps"], g.times(1))
                sp.dma_start(c_in[:], cg[:, bass.ds(g.times(4), G), :]).then_inc(s["c_inn"], 16)

            def load_x(i, b0, b1):
                sp.dma_start(xr[:, b0:b1, :], xg[:, b0:b1, :]).then_inc(s[f"x_in{i}"], 16)

            load_ctx(At(0, mult=1))
            sp.dma_start(wk_raw[:], Wk).then_inc(s["wk_in"], 16)
            sp.dma_start(wq_raw[:], Wq).then_inc(s["wq_in"], 16)
            for col, b in ((bk_col, bk), (bq_col, bq)):
                sp.dma_start(col[:], b.rearrange("(h d o) -> d h o", d=DH, o=1), allow_slow_non_contiguous=True
                             ).then_inc(s["b_in"], 16)
            sp.dma_start(wg_raw[:], w_g).then_inc(s["g_in"], 16)
            load_x(0, 0, G)
            sp.dma_start(wv_s[:], Wv).then_inc(s["v_in"], 16)
            sp.dma_start(bv_all[:], bv.partition_broadcast(P)).then_inc(s["v_in"], 16)
            sp.dma_start(bo_all[:], bo.partition_broadcast(P)).then_inc(s["o_in"], 16)
            sp.dma_start(wo_s[:], Wo).then_inc(s["o_in"], 16)
            load_x(1, G, 2 * G)
            load_ctx(At(1, mult=1))
            load_x(2, 2 * G, B)

            def store(g, parts, stack, done, put_, terms):
                for part, ready in enumerate(done):
                    at = [t for t in range(NT) if terms[t] == part]
                    step_ = at[1] - at[0] if len(at) > 1 else 1
                    need(sp, s[ready], g.times(1, 1))
                    settle(sp)
                    sp.dma_start(stack[bass.ds(g.times(1), 1), at[0]:at[-1] + 1:step_, :, :]
                                 .rearrange("o t r q -> (o r) t q"),
                                 parts[:, part, :].unsqueeze(1).to_broadcast([P, len(at), G * S])
                                 ).then_inc(s[put_], 16)

            def store_k(g):
                store(g, kp, k_stack_d, ("k1", "k2", "k3"), "k_put", K_TERMS)

            def store_q(g):
                store(g, qp, q_stack_d, ("q1", "q2", "q3"), "q_put", Q_TERMS)

            def load_stacks(b, u, r):
                if not live(b):
                    return
                i = b.base % 4
                if u == 1 or b.known and b.base == 0:
                    g = r + 1
                    sp.wait_ge(s["q_put"], g.times(STORED, STORED))
                    settle(sp)
                    sp.wait_ge(s["k_put"], g.times(STORED, STORED))
                    settle(sp)
                need(sp, s["s2"], b.times(4, -12))
                settle(sp)
                row = bass.ds(b.group(), 1)
                cols = slice(i * S, (i + 1) * S)
                for t, src, got in ((qs, q_stack_d, q_in), (km, k_stack_d, km_in), (ks, k_stack_d, k_in)):
                    sp.dma_start(t[i][0:KR, :].rearrange("r (h q) -> r h q", h=H),
                                 src[row, :, :, cols].rearrange("o t (d h) q -> (o t d) h q", d=DH)
                                 ).then_inc(got[i], 16)

            def max_rows(b):
                if not live(b):
                    return
                i = b.base % 4
                sp.wait_ge(s["nT_out"], b.times(1, 1))
                sp.dma_start(qs[i][KR:KR + 3, :].rearrange("t (h q) -> t h q", h=H), nT[i][:]).then_inc(m_in[i], 16)

            sp.wait_ge(s["e_ready"], 1)
            slot_parts = slots_d.rearrange("(q p a b) w -> q p a (b w)", q=FILLS, p=P, b=4)

            filled = iter(range(FILLS))

            def fill(n):
                for q in list(islice(filled, n)):
                    sp.dma_start(slot_parts[q],
                                 empty[:].rearrange("p b w -> p (b w)").unsqueeze(1)
                                 .to_broadcast([P, E * 2 * CAP // P // 4 // FILLS, 4 * RW])).then_inc(s["fills"], 16)

            fill(12)
            for g in range(2):
                store_k(At(g, mult=1))
                store_q(At(g, mult=1))
                if g == 0:
                    sp.wait_ge(s["zeroed"], 7)
                else:
                    sp.wait_ge(s["zeroed3"], 6)
                sp.wait_ge(s["c_ready"], 1)
                for i in (2 * g, 2 * g + 1):
                    sp.dma_start(ks[i][KR:KR + 3, :], ones_rows[:]).then_inc(k_in[i], 16)
                if g == 0:
                    load_stacks(At(0), 0, At(-1, mult=1))
                    load_stacks(At(1), 0, None)
                    load_ctx(At(2, mult=1))
            res_parts = result_d.rearrange("(q p a b) d -> q p a (b d)", q=NG, p=P, b=4)

            def step(j, u, r):
                if not (j.known and j.base < -1):
                    load_stacks(j + 3, u, r)
                max_rows(j + 1)
                if j.known:
                    fill(STEP_FILLS)
                g, before_g = group_of(r), group_of(r + (-1))
                if u == 0 and before_g is not None:
                    store_q(before_g)
                if u == 1 and g is not None and not (g.known and g.base >= NG - 1):
                    load_ctx(g + 1)
                if u == 3 and g is not None:
                    store_k(g)
                if u == 2 and (not r.known or 0 <= r.base < NG):
                    sp.dma_start(res_parts[bass.ds(r.times(1), 1)].rearrange("o p a w -> (o p) a w"),
                                 zeros[:].rearrange("p b w -> p (b w)").unsqueeze(1)
                                 .to_broadcast([P, TOP_K * N // P // 4 // NG, 4 * D])).then_inc(s["rfills"], 16)

            steps(sp, step, (STORED,))
            assert next(filled, None) is None

            def load_weights(e):
                sp.dma_start(w1[:], c_fc[bass.ds(e, 1)].rearrange("o c f -> (o c) f")).then_inc(s["w1_in"], 16)
                sp.dma_start(w2[:].rearrange("p (n c) -> p n c", n=NF),
                             c_proj[bass.ds(e, 1)].rearrange("o (n f) c -> (o f) n c", n=NF)
                             ).then_inc(s["w2_in"], 16)

            load_weights(0)
            sp.wait_ge(s["starts_done"], 1)
            sp.wait_ge(s["sc1"], 16 * TOP_K * B)
            window = {}

            def load(of, u):
                need(sp, put[u % NCH], of(64, 32 * (u // NCH) - 32))
                if u % NCH == 0:
                    window[0] = nc.values_load(starts[0:1, bass.ds(of(2, u // NCH), 1)], [mybir.EngineType.SP],
                                               min_val=0, max_val=(2 * E - 1) * CAP,
                                               skip_runtime_bounds_check_because="the number of first choices "
                                               "in it is clamped to 0 .. CAP")
                sp.dma_start(br[u], slots_d[bass.ds(window[0] + u % NCH * CH, CH), :]
                             .rearrange("(t p) w -> p t w", p=P)).then_inc(br_in[u], 16)
                if u % NCH == 1:
                    e = next_expert(sp, of, u // NCH + 1)
                    sp.wait_ge(s["w_low"], of(4, 2 * (u // NCH) + 2))
                    load_weights(e)

            chunks(sp, load)
            sp.wait_ge(s["w1_in"], 16 * (E + 1))
            sp.wait_ge(s["w2_in"], 16 * (E + 1))

            for i in range(NCH):
                sp.wait_ge(put[i], 32 * E)
            res = result_d.rearrange("(k g t p) d -> k g p t d", k=TOP_K, t=G, p=P)
            outg = out.rearrange("(g t) s d -> g s t d", t=G)
            for g in range(NG + YR - 1):
                if g < NG:
                    need(sp, s["summed"], g - YR + 1)
                    for k in range(TOP_K):
                        sp.dma_start(ya[g % YR][k], res[k, g]).then_inc(ya_in[g % YR], 16)
                h = g - YR + 1
                if h >= 0:
                    sp.wait_ge(s["summed"], h + 1)
                    sp.dma_start(outg[h], xr[:, G * h:G * (h + 1), :]).then_inc(out_put[h % YR], 16)
            for i in range(YR):
                sp.wait_ge(out_put[i], 16 * NG // YR)

        @block.gpsimd
        def _(pool):
            pool.memset(ident[:], 0.0).then_inc(s["rt"], 1)
            pool.memset(mhalf[:], -0.5).then_inc(s["rt"], 1)
            pool.wait_ge(s["empty0"], 1)
            pool.iota(empty[:, :, D:D + 1].bitcast(I32), [[0, 4], [0, 1]], base=TOP_K * N + FAR,
                      channel_multiplier=0).then_inc(s["e_ready"], 1)
            pool.wait_ge(s["rt"], 2)
            pool.affine_select(out=ident[:], in_=ident[:], compare_op=ALU.not_equal, fill=1.0, base=0,
                               pattern=[[-1, P]], channel_multiplier=1).then_inc(s["rt"], 1)
            for w, r, got in ((wk_s, wk_raw, "wk_in"), (wq_s, wq_raw, "wq_in")):
                pool.wait_ge(s[got], 16)
                pool.tensor_copy(w[:].rearrange("p (d h) -> p d h", d=DH),
                                 r[:].rearrange("p (h d) -> p d h", d=DH)).then_inc(s["wperm"], 1)

            def deviations(g):
                pool.wait_ge(s["mvA_done"], g.times(4, G))
                need(pool, s["rstdA_done"], g.times(1))
                settle(pool)
                pool.tensor_scalar(vareA[:], mvA[:, :, 1], EPS, None, ALU.add).then_inc(s["vareA_done"], 1)
                pool.wait_ge(s["vareA_done"], g.times(1, 1))
                need(pool, s["xnA_done"], g.times(4))
                pool.tensor_tensor(rstdA[:], vareA[:], mhalf[:], ALU.pow).then_inc(s["rstdA_done"], 1)

            def add_bias(g):
                pool.wait_ge(s["xnA_done"], g.times(4, G))
                if g.known and g.base == 0:
                    pool.wait_ge(s["o_in"], 32)
                xg = xr[:, bass.ds(g.times(4), G), :]
                pool.tensor_tensor(xg, xg, bo_all[:].unsqueeze(1).to_broadcast([P, G, D]), ALU.add
                                   ).then_inc(s["xbo"], 1)

            def third_k(g):
                pool.wait_ge(s["k2"], g.times(1, 1))
                need(pool, s["k_put"], g.times(STORED))
                pool.tensor_tensor(kp[:, 2, :], kr[:], kp[:, 1, :], ALU.subtract).then_inc(s["k3"], 1)

            def third_q(g):
                pool.wait_ge(s["q2"], g.times(1, 1))
                need(pool, s["q_put"], g.times(STORED))
                pool.tensor_tensor(qp[:, 2, :], qr[:], qp[:, 1, :], ALU.subtract).then_inc(s["q3"], 1)

            first, second = At(0, mult=1), At(1, mult=1)
            deviations(first)
            add_bias(first)
            deviations(second)
            pool.wait_ge(s["rt"], 3)
            pool.tensor_copy(identb[:], ident[:]).then_inc(s["rt"], 1)
            pool.memset(ones_rows[:], 1.0).then_inc(s["rt"], 1)
            pool.wait_ge(s["rt"], 5)
            pool.sem_inc(s["c_ready"], 1)
            third_k(first)
            for t in (qs[2], km[2], ks[2], qs[3], km[3], ks[3]):
                pool.memset(t[:].bitcast(U32), 0).then_inc(s["zeroed3"], 1)
            third_q(first)
            add_bias(second)
            third_k(second)
            third_q(second)
            deviations(At(2, mult=1))

            pool.memset(before[:], 1.0).then_inc(s["rt"], 1)
            pool.memset(onesb[:], 1.0).then_inc(s["rt"], 1)
            pool.memset(cap_g[:], float(2 * CAP)).then_inc(s["rt"], 1)
            pool.memset(turn_g[:, :, 0:1], -1.0).then_inc(s["rt"], 1)
            pool.memset(turn_g[:, :, 1:2], 1.0).then_inc(s["rt"], 1)
            pool.memset(mid_g[:, :, 0:1], float(CAP - 1)).then_inc(s["rt"], 1)
            pool.memset(mid_g[:, :, 1:2], float(CAP)).then_inc(s["rt"], 1)
            pool.iota(window0[:], [[2 * CAP, E]], base=CAP, channel_multiplier=0,
                      allow_small_or_imprecise_dtypes=True).then_inc(s["rt"], 1)
            pool.memset(carry[:], 0.0).then_inc(s["rt"], 1)
            pool.memset(stage[:, :, :, D + 1:RW], 0.0).then_inc(s["rt"], 1)
            pool.iota(ids[:], [[N, TOP_K], [P, B]], base=0, channel_multiplier=1).then_inc(s["rt"], 1)
            pool.iota(ioE[:], [[1, E]], base=0, channel_multiplier=0,
                      allow_small_or_imprecise_dtypes=True).then_inc(s["rt"], 1)
            pool.wait_ge(s["rt"], 17)
            pool.affine_select(out=before[:], in_=before[:], compare_op=ALU.is_gt, fill=0.0, base=0,
                               pattern=[[1, P]], channel_multiplier=-1).then_inc(s["rt"], 1)
            pool.wait_ge(s["rt"], 18)
            pool.sem_inc(s["c_ready"], 1)

            def v_beside_ones(b):
                if not live(b):
                    return
                pool.wait_ge(s["v_out"], b.group() + 1)
                need(pool, s["av"], b.times(4, -4))
                if b.known and b.base < 2:
                    pool.wait_ge(s["zeroed"], 11)
                pool.tensor_copy(va[b.base % 2][:, :, 0:DH],
                                 v_all[:, bass.ds(b.times(1), 1), :].rearrange("p o (h d) -> p (o h) d", d=DH)
                                 ).then_inc(s["va_in"], 1)

            def deviation(b):
                if not live(b):
                    return
                pool.wait_ge(s["mv_done"], b.times(1, 1))
                settle(pool)
                pool.tensor_scalar(vare[:], mv[:, 1:2], EPS, None, ALU.add).then_inc(s["vare_done"], 1)
                pool.wait_ge(s["vare_done"], b.times(1, 1))
                need(pool, s["xs_done"], b.times(1))
                pool.tensor_tensor(rstd[:], vare[:], mhalf[:, 0:1], ALU.pow).then_inc(s["rstd_done"], 1)

            def slots_of_group(q):
                cols = bass.ds(q.times(4), G)
                pool.wait_ge(s["rkg_done"], q.times(1, 1))
                pool.tensor_tensor(rkm[:], rkg[:], ohg[:], ALU.mult).then_inc(s["rkm_done"], 1)
                pool.wait_ge(s["rkm_done"], q.times(1, 1))
                m = rkm[:].rearrange("p g (k e) -> p (g k) e", e=E)
                pool.tensor_tensor(m[:, :, 0:4], m[:, :, 0:4], m[:, :, 4:8], ALU.add).then_inc(s["rankg_done"], 1)
                pool.wait_ge(s["rankg_done"], q.times(3, 1))
                pool.tensor_tensor(m[:, :, 0:2], m[:, :, 0:2], m[:, :, 2:4], ALU.add).then_inc(s["rankg_done"], 1)
                pool.wait_ge(s["rankg_done"], q.times(3, 2))
                pool.tensor_tensor(rankg[:].rearrange("p g k -> p (g k)").unsqueeze(2), m[:, :, 0:1], m[:, :, 1:2],
                                   ALU.add).then_inc(s["rankg_done"], 1)
                pool.tensor_tensor(slotg[:], ti[:, :, cols].rearrange("p k g -> p g k"), cap_g[:], ALU.mult
                                   ).then_inc(s["slotg_done"], 1)
                pool.wait_ge(s["rankg_done"], q.times(3, 3))
                pool.tensor_copy(ranks[:, :, cols].rearrange("p k g -> p g k"), rankg[:]).then_inc(s["skipg"], 1)
                pool.tensor_tensor(away[:], rankg[:], turn_g[:], ALU.mult).then_inc(s["skipg"], 1)
                pool.wait_ge(s["slotg_done"], q.times(4, 1))
                pool.tensor_tensor(slotg[:], slotg[:], mid_g[:], ALU.add).then_inc(s["slotg_done"], 1)
                settle(pool)
                pool.tensor_scalar(skip[:], rankg[:], float(CAP), float(FAR), ALU.is_ge, ALU.mult
                                   ).then_inc(s["skipg"], 1)
                pool.wait_ge(s["skipg"], q.times(4, 3))
                pool.tensor_tensor(away[:], away[:], skip[:], ALU.add).then_inc(s["skipg"], 1)
                pool.wait_ge(s["skipg"], q.times(4, 4))
                pool.wait_ge(s["slotg_done"], q.times(4, 2))
                pool.tensor_tensor(slotg[:], slotg[:], away[:], ALU.add).then_inc(s["slotg_done"], 1)
                pool.wait_ge(s["slotg_done"], q.times(4, 3))
                need(pool, s["sc1"], q.times(SCATTERED))
                settle(pool)
                pool.tensor_copy(slotig[:], slotg[:]).then_inc(s["slotg_done"], 1)
                for k in range(TOP_K):
                    pool.tensor_copy(stage[:, k, :, D:D + 1].bitcast(I32), ids[:, k, cols].unsqueeze(2)
                                     ).then_inc(s["ids_staged"], 1)

            def scatter_group(q, rows_):
                if 0 in rows_ and q.known and q.base == 0:
                    pool.wait_ge(s["fills"], 16 * FILLS)
                if 0 in rows_:
                    pool.wait_ge(s["staged"], q.times(2, 2))
                    pool.wait_ge(s["ids_staged"], q.times(2, 2))
                    pool.wait_ge(s["slotg_done"], q.times(4, 4))
                    settle(pool)
                for row in rows_:
                    t, k = row // TOP_K, row % TOP_K
                    pool.indirect_dma_start(slots_d, bass.IndirectOffsetOnAxis(ap=slotig[:, t, k:k + 1], axis=0),
                                            stage[:, k, t, :], None, bounds_check=E * 2 * CAP - 1, oob_is_err=False
                                            ).then_inc(s["sc1"], 16)

            def step(j, u, r):
                g, to_scatter = group_of(r), ranked(r + (-1))
                deviation(j + (-2))
                if u == 0 and group_of(r + (-1)) is not None:
                    third_q(group_of(r + (-1)))
                v_beside_ones(j + 1)
                if u == 1 and g is not None:
                    add_bias(g)
                if u == 1 and to_scatter is not None:
                    scatter_group(to_scatter, (0, 1, 2))
                if u == 3 and g is not None:
                    third_k(g)
                if u == 2 and to_scatter is not None:
                    scatter_group(to_scatter, (3, 4))
                if u == 3 and to_scatter is not None:
                    scatter_group(to_scatter, (6, 7))
                if u == 3 and g is not None and not (g.known and g.base >= NG - 1):
                    deviations(g + 1)
                if u == 2 and to_scatter is not None:
                    scatter_group(to_scatter, (5,))
                if u == 0 and to_scatter is not None:
                    slots_of_group(to_scatter)

            steps(pool, step, (3, 12, SCATTERED, STORED, 2))

            slots_of_group(At(NG - 1, mult=1))
            scatter_group(At(NG - 1, mult=1), range(TOP_K * G))
            pool.wait_ge(s["rfills"], 16 * NG)

            def scatter(of, u):
                if there(of, u - 5):
                    v = u - 5
                    pool.wait_ge(s["y_out"], of(2 * NCH, v + 1))
                    settle(pool)
                    for t in range(2):
                        pool.indirect_dma_start(result_d, bass.IndirectOffsetOnAxis(
                                                    ap=br[v % (2 * NCH)][:, t, D:D + 1].bitcast(I32), axis=0),
                                                ys[v % NCH][:, t, :], None, bounds_check=TOP_K * N - 1,
                                                oob_is_err=False).then_inc(put[v % NCH], 16)
                if there(of, u - 1):
                    v = u - 1
                    pool.wait_ge(s["hr_done"], of(4 * NCH, 2 * v + 2))
                    need(pool, s["hl_done"], of(2 * NCH, v - 1))
                    pool.tensor_tensor(sq[v % 2][:, SQ:], hr[v % 2][:, SQ:], hr[v % 2][:, SQ:], ALU.mult
                                       ).then_inc(s["sq2_done"], 1)

            chunks(pool, scatter, 5)

        @block.scalar
        def _(act):
            def ctx_turned(g):
                act.wait_ge(s["cT_ps"], g.times(1, 1))
                need(act, s["v_ps"], g.times(1))
                act.copy(cTA[:], bank[6][:]).then_inc(s["cT_out"], 1)

            def first_k(g):
                act.wait_ge(s["k_ps"], g.times(1, 1))
                need(act, s["k_put"], g.times(STORED))
                act.activation(kp[:, 0, :], bank[6][:], ACT.Identity, bias=bk_col[:]).then_inc(s["k1"], 1)

            def second_k(g):
                act.wait_ge(s["kr_done"], g.times(1, 1))
                act.copy(kp[:, 1, :], kr[:]).then_inc(s["k2"], 1)

            def x_turned(g):
                act.wait_ge(s["xT_ps"], g.times(1, 1))
                need(act, s["q_ps"], g.times(1))
                act.copy(xTA[:], bank[6][:]).then_inc(s["xT_out"], 1)

            def first_q(g):
                act.wait_ge(s["q_ps"], g.times(1, 1))
                need(act, s["q_put"], g.times(STORED))
                act.activation(qp[:, 0, :], bank[6][:], ACT.Identity, bias=bq_col[:]).then_inc(s["q1"], 1)

            def second_q(g):
                act.wait_ge(s["qr_done"], g.times(1, 1))
                act.copy(qp[:, 1, :], qr[:]).then_inc(s["q2"], 1)

            first, second = At(0, mult=1), At(1, mult=1)
            ctx_turned(first)
            act.wait_ge(s["b_in"], 32)
            first_k(first)
            act.wait_ge(s["wgT_ps"], 1)
            act.copy(wgT[:], bank[7][:, 0:E]).then_inc(s["wgT_out"], 1)
            for part in (x_turned, second_k, first_q, second_q):
                part(first)
            for part in (ctx_turned, first_k, x_turned, second_k, first_q, second_q):
                part(second)

            def exps(b, c):
                if not live(b):
                    return
                act.wait_ge(s["s2"], b.times(4, c + 1))
                need(act, s["av"], b.times(4, c - 3))
                act.activation(pr[c][:], bank[2 + c % 2][:], ACT.Exp, scale=SCALE).then_inc(s["ex"], 1)

            def maxima_out(b):
                if not live(b):
                    return
                act.wait_ge(s["nT_ps"], b.times(1, 1))
                i = b.base % 4
                need(act, m_in[i], b.rounds16(-16))
                act.copy(nT[i][:], bank[7][0:3 * H, 0:S // 2].bitcast(BF16)).then_inc(s["nT_out"], 1)

            def keep_residual(b):
                if not live(b):
                    return
                act.wait_ge(s["x1_done"], b.times(1, 1))
                act.copy(xr[:, bass.ds(b.times(1), 1), :], x1[b.base % 2][:].unsqueeze(1)).then_inc(s["x1_kept"], 1)

            def keep_normed(b):
                if not live(b):
                    return
                act.wait_ge(s["xs_done"], b.times(1, 1))
                act.copy(rows[:, bass.ds(b.times(1), 1), :], xs[b.base % 2][:].unsqueeze(1)
                         ).then_inc(s["xs_kept"], 1)

            def keep_top(b):
                if not live(b):
                    return
                act.wait_ge(s["idx_done"], b.times(1, 1))
                col = bass.ds(b.times(1), 1)
                act.copy(tv[:, :, col], top8[:, 0:TOP_K].unsqueeze(2)).then_inc(s["top_kept"], 1)
                act.copy(ti[:, :, col], idx8[:, 0:TOP_K].unsqueeze(2)).then_inc(s["top_kept"], 1)

            def stage_group(q):
                act.wait_ge(s["xs_kept"], q.times(4, 4))
                need(act, s["sc1"], q.times(SCATTERED))
                for k in range(TOP_K):
                    act.copy(stage[:, k, :, 0:D], rows[:, bass.ds(q.times(4), G), :]).then_inc(s["staged"], 1)

            def normed_out(b):
                if not live(b):
                    return
                act.wait_ge(s["xsT_ps"], b.times(1, 1))
                need(act, s["lg"], b.times(1))
                act.copy(xsT[:], bank[7][:, 128:256]).then_inc(s["xsT_out"], 1)

            def context_out(b):
                if not live(b):
                    return
                act.wait_ge(s["cnT_ps"], b.times(1, 1))
                need(act, s["wo_ps"], b.times(1))
                act.copy(cnT[:], bank[5][:, 0:128]).then_inc(s["cnT_out"], 1)

            def weighted_out(b):
                if not live(b):
                    return
                act.wait_ge(s["av"], b.times(4, 4))
                need(act, s["nat"], b.times(1))
                act.copy(avs[:], bank[4][:]).then_inc(s["av_out"], 1)

            def step(j, u, r):
                g = group_of(r)
                keep_top(j + (-4))
                exps(j, 0)
                keep_normed(j + (-3))
                if u == 1 and ranked(r + (-1)) is not None:
                    stage_group(ranked(r + (-1)))
                if u == 3 and g is not None:
                    first_q(g)
                maxima_out(j + 1)
                if u == 1 and g is not None:
                    first_k(g)
                if u == 2 and g is not None:
                    x_turned(g)
                exps(j, 1)
                keep_residual(j + (-2))
                exps(j, 2)
                if u == 0 and g is not None:
                    ctx_turned(g)
                context_out(j + (-1))
                exps(j, 3)
                if u == 2 and g is not None:
                    second_k(g)
                weighted_out(j)
                if u == 3 and g is not None:
                    second_q(g)
                normed_out(j + (-2))

            steps(act, step, (STORED, SCATTERED))
            stage_group(At(NG - 1, mult=1))

            act.wait_ge(s["rt2"], 2)
            act.activation(pe2[:], pdiff[:], ACT.Exp).then_inc(s["pe_done"], 1)

            def weights_high(of, x, j):
                act.wait_ge(s[f"w{j + 1}_in"], of(32, 16 * x + 16))
                need(act, s["y_ps"], of(2 * NCH, NCH * (x - 1)))
                act.copy((w1h, w2h)[j][x % 2][:], (w1, w2)[j][:]).then_inc(s["w_high"], 1)

            for j in range(2):
                weights_high(lambda k, plus: plus, 0, j)

            def hidden(of, u):
                if there(of, u - 4):
                    v = u - 4
                    act.wait_ge(s["y_ps"], of(2 * NCH, v + 1))
                    need(act, s["back_ps"], of(2 * NCH, v - 1))
                    act.copy(yT[v % 2][:], bank[6][:, 0:CH]).then_inc(s["yT_out"], 1)
                if there(of, u):
                    act.wait_ge(s["bT_ps"], of(2 * NCH, u + 1))
                    need(act, s["h_ps"], of(4 * NCH, 2 * u - 2))
                    act.copy(bTh[u % 2][:], bank[u % 2][:, 0:CH]).then_inc(s["bT_high"], 1)
                if there(of, u - 1):
                    v = u - 1
                    need(act, s["sq_done"], of(2 * NCH, v - 1))
                    need(act, s["sq2_done"], of(2 * NCH, v - 1))
                    need(act, s["hh_done"], of(2 * NCH, v - 1))
                    for half in range(2):
                        act.wait_ge(s["h_ps"], of(4 * NCH, 2 * v + 1 + half))
                        act.activation(hr[v % 2][:, half * 2 * CH:(half + 1) * 2 * CH],
                                       bank[2 + 2 * (v % 2) + half][:], ACT.Relu).then_inc(s["hr_done"], 1)
                if 2 <= u % NCH <= 3 and there(of, u):
                    weights_high(of, u // NCH + 1, u % NCH - 2)
                if there(of, u - 1):
                    v = u - 1
                    act.wait_ge(s["hr_done"], of(4 * NCH, 2 * v + 2))
                    need(act, s["y_ps"], of(2 * NCH, v - 1))
                    act.activation(hh[v % 2][:], hr[v % 2], ACT.Square).then_inc(s["hh_done"], 1)

            chunks(act, hidden, 4)

            act.wait_ge(s["prob_done"], 2)
            for g in range(NG):
                act.wait_ge(ya_in[g % YR], 32 * (g // YR + 1))
                for t in range(G):
                    y = ya[g % YR][0][:, t, :]
                    act.activation(y, y, ACT.Copy, scale=prob[:, 0, G * g + t:G * g + t + 1]
                                   ).then_inc(s["weighted"], 1)

        @block.vector
        def _(dve):
            dve.memset(empty[:], 0.0).then_inc(s["empty0"], 1)
            dve.memset(zeros[:], 0.0).then_inc(s["zeroed"], 1)

            def clear(t):
                flat = t[:] if len(t[:].shape) == 2 else t[:].rearrange("p h w -> p (h w)")
                dve.memset(flat.bitcast(U32), 0).then_inc(s["zeroed"], 1)

            def row_x(g, t):
                return xr[:, bass.ds(g.times(4, t), 1), :].rearrange("p o d -> p (o d)")

            def statistics(g):
                dve.wait_ge(s[f"x_in{min(g.base, 2) if g.known else 2}"], 16)
                need(dve, s["mvA_done"], g.times(4))
                settle(dve)
                for t in range(G):
                    dve.bn_stats(stA[:, t, :], row_x(g, t)).then_inc(s["stA_done"], 1)

            def moments(g):
                need(dve, s["xnA_done"], g.times(4))
                dve.wait_ge(s["stA_done"], g.times(4, G))
                settle(dve)
                for t in range(G):
                    dve.bn_aggr(mvA[:, t, :], stA[:, t, :]).then_inc(s["mvA_done"], 1)

            def norm(g):
                dve.wait_ge(s["rstdA_done"], g.times(1, 1))
                need(dve, s["xT_ps"], g.times(1))
                for t in range(G):
                    dve.tensor_scalar(xnA[:, t, :], row_x(g, t), mvA[:, t, 0:1], rstdA[:, t:t + 1],
                                      ALU.subtract, ALU.mult).then_inc(s["xnA_done"], 1)

            def v_rows(g):
                dve.wait_ge(s["v_ps"], g.times(1, 1))
                dve.tensor_tensor(v_all[:, bass.ds(g.times(4), G), :],
                                  bank[6][:].rearrange("p (g d) -> p g d", g=G),
                                  bv_all[:].unsqueeze(1).to_broadcast([P, G, D]), ALU.add).then_inc(s["v_out"], 1)

            def rest_k(g):
                dve.wait_ge(s["k1"], g.times(1, 1))
                need(dve, s["k3"], g.times(1))
                dve.scalar_tensor_tensor(out=kr[:], in0=bank[6][:], scalar=bk_col[:], in1=kp[:, 0, :],
                                         op0=ALU.add, op1=ALU.subtract).then_inc(s["kr_done"], 1)

            def rest_q(g):
                dve.wait_ge(s["q1"], g.times(1, 1))
                need(dve, s["q3"], g.times(1))
                dve.scalar_tensor_tensor(out=qr[:], in0=bank[6][:], scalar=bq_col[:], in1=qp[:, 0, :],
                                         op0=ALU.add, op1=ALU.subtract).then_inc(s["qr_done"], 1)

            for t in (qs[0], km[0], ks[0]):
                clear(t)
            first, second = At(0, mult=1), At(1, mult=1)
            statistics(first)
            moments(first)
            norm(first)
            statistics(second)
            moments(second)
            rest_k(first)
            dve.wait_ge(s["v_in"], 32)
            v_rows(first)
            for t in (qs[1], km[1], ks[1]):
                clear(t)
            norm(second)
            rest_q(first)
            statistics(At(2, mult=1))
            moments(At(2, mult=1))
            rest_k(second)
            v_rows(second)
            for t in va:
                clear(t)
            rest_q(second)
            dve.wait_ge(s["zeroed"], 9)
            for t in va:
                dve.memset(t[:, :, DH:DH + 1], 1.0).then_inc(s["zeroed"], 1)

            def maxes(b, c):
                if not live(b):
                    return
                dve.wait_ge(s["s1"], b.times(4, c + 1))
                if c == 0:
                    need(dve, s["nr"], b.times(1, -1))
                dve.tensor_reduce(mxt[b.base % 2][:, HC * c:HC * c + HC],
                                  bank[c % 2][:].rearrange("p (h k) -> p h k", h=HC), AX.X, ALU.max
                                  ).then_inc(s["mx"], 1)

            nat = bank[5][:].rearrange("p (h w) -> p h w", h=H)

            def sums(b):
                if not live(b):
                    return
                dve.wait_ge(s["nat"], b.times(1, 1))
                need(dve, s["cn_done"], b.times(1))
                dve.reciprocal(rden[:].unsqueeze(2), nat[:, :, DH:DH + 1]).then_inc(s["rec"], 1)

            def normal_context(b):
                if not live(b):
                    return
                need(dve, s["cnT_ps"], b.times(1))
                dve.wait_ge(s["rec"], b.times(1, 1))
                dve.tensor_tensor(cn[:].rearrange("p (h d) -> p h d", h=H), nat[:, :, 0:DH],
                                  rden[:].unsqueeze(2).to_broadcast([P, H, DH]), ALU.mult
                                  ).then_inc(s["cn_done"], 1)

            logits = bank[7][:, 256:256 + E]

            def top_values(b):
                if not live(b):
                    return
                dve.wait_ge(s["lg"], b.times(1, 1))
                need(dve, s["top_kept"], twice(b))
                settle(dve)
                dve.max(out=top8[:], in_=logits).then_inc(s["top_done"], 1)

            def top_experts(b):
                if not live(b):
                    return
                dve.wait_ge(s["top_done"], b.times(1, 1))
                settle(dve)
                dve.max_index(out=idx8[:], in_max=top8[:], in_values=logits).then_inc(s["idx_done"], 1)

            def residual(b):
                if not live(b):
                    return
                i = b.base % 2
                dve.wait_ge(s["wo_ps"], b.times(1, 1))
                need(dve, s["x1_kept"], b.times(1, -1))
                need(dve, s["xs_done"], b.times(1, -1))
                if b.known and b.base == 0:
                    dve.wait_ge(s["xbo"], 1)
                dve.tensor_tensor(x1[i][:].unsqueeze(1), bank[5][:, 128:256].unsqueeze(1),
                                  xr[:, bass.ds(b.times(1), 1), :], ALU.add).then_inc(s["x1_done"], 1)

            def residual_statistics(b):
                if not live(b):
                    return
                dve.wait_ge(s["x1_done"], b.times(1, 1))
                need(dve, s["mv_done"], b.times(1))
                dve.bn_stats(st[:], x1[b.base % 2][:]).then_inc(s["st_done"], 1)

            def residual_moments(b):
                if not live(b):
                    return
                dve.wait_ge(s["st_done"], b.times(1, 1))
                need(dve, s["xs_done"], b.times(1))
                settle(dve)
                dve.bn_aggr(mv[:], st[:]).then_inc(s["mv_done"], 1)

            def negative_max(b, part):
                if not live(b):
                    return
                if part == 0:
                    need(dve, s["nT_ps"], b.times(1))
                    dve.wait_ge(s["mx"], b.times(4, 4))
                    dve.tensor_scalar(nparts[:, 0, :], mxt[b.base % 2][:], -1.0, None, ALU.mult).then_inc(s["n1"], 1)
                if part == 1:
                    dve.wait_ge(s["n1"], b.times(1, 1))
                    dve.scalar_tensor_tensor(out=nrem[:], in0=mxt[b.base % 2][:], scalar=-1.0, in1=nparts[:, 0, :],
                                             op0=ALU.mult, op1=ALU.subtract).then_inc(s["nr"], 1)
                if part == 2:
                    dve.wait_ge(s["nr"], b.times(1, 1))
                    dve.tensor_copy(nparts[:, 1, :], nrem[:]).then_inc(s["n2"], 1)
                if part == 3:
                    dve.wait_ge(s["n2"], b.times(1, 1))
                    dve.tensor_tensor(nparts[:, 2, :], nrem[:], nparts[:, 1, :], ALU.subtract).then_inc(s["n3"], 1)

            def normed(b):
                if not live(b):
                    return
                i = b.base % 2
                dve.wait_ge(s["rstd_done"], b.times(1, 1))
                need(dve, s["xsT_ps"], b.times(1, -1))
                need(dve, s["xs_kept"], b.times(1, -1))
                dve.tensor_scalar(xs[i][:], x1[i][:], mv[:, 0:1], rstd[:], ALU.subtract, ALU.mult
                                  ).then_inc(s["xs_done"], 1)

            def one_hot_group(q):
                dve.wait_ge(s["top_kept"], q.times(8, 8))
                need(dve, s["rkm_done"], q.times(1))
                if q.known and q.base == 0:
                    dve.wait_ge(s["c_ready"], 2)
                for k in range(TOP_K):
                    dve.tensor_tensor(ohg[:, :, k * E:(k + 1) * E],
                                      ti[:, k, bass.ds(q.times(4), G)].unsqueeze(2).to_broadcast([P, G, E]),
                                      ioE[:].unsqueeze(1).to_broadcast([P, G, E]), ALU.is_equal
                                      ).then_inc(s["ohg_done"], 1)

            gr = bank[6][:, 0:(G + 1) * TOP_K * E].rearrange("p (t e) -> p t e", e=TOP_K * E)

            def rank_group(q):
                dve.wait_ge(s["rkg_ps"], q.times(1, 1))
                need(dve, s["carried"], q.times(1))
                need(dve, s["rkm_done"], q.times(1))
                dve.tensor_tensor(rkg[:], gr[:, 0:G, :], carry[:].unsqueeze(1).to_broadcast([P, G, TOP_K * E]), ALU.add
                                  ).then_inc(s["rkg_done"], 1)

            def carry_group(q):
                dve.wait_ge(s["rkg_done"], q.times(1, 1))
                dve.tensor_tensor(carry[:].unsqueeze(1), carry[:].unsqueeze(1), gr[:, G:G + 1, :], ALU.add
                                  ).then_inc(s["carried"], 1)

            def step(j, u, r):
                g, q = group_of(r), ranked(r)
                ahead, last, second, third = j + 2, j + (-1), j + (-2), j + (-3)
                negative_max(j + 1, 0)
                maxes(ahead, 0)
                negative_max(j + 1, 1)
                residual(second)
                negative_max(j + 1, 2)
                if u == 3 and q is not None:
                    one_hot_group(q)
                negative_max(j + 1, 3)
                residual_statistics(second)
                maxes(ahead, 1)
                residual_moments(second)
                sums(last)
                if u == 0 and g is not None:
                    norm(g)
                normal_context(last)
                if u == 1 and g is not None:
                    rest_k(g)
                maxes(ahead, 2)
                if u == 3 and g is not None:
                    rest_q(g)
                if u == 2 and g is not None and not (g.known and g.base >= NG - 1):
                    statistics(g + 1)
                top_values(third)
                normed(second)
                if u == 3 and g is not None and not (g.known and g.base >= NG - 1):
                    moments(g + 1)
                top_experts(third)
                if u == 3 and q is not None:
                    rank_group(q)
                maxes(ahead, 3)
                if u == 1 and g is not None:
                    v_rows(g)
                if u == 3 and q is not None:
                    carry_group(q)

            steps(dve, step, (3, 8, 2))

            n = [0]

            def link(ins):
                n[0] += 1
                ins.then_inc(s["rt2"], 1)
                dve.wait_ge(s["rt2"], n[0])

            dve.wait_ge(s["carried"], NG)
            link(dve.tensor_scalar(firsts[:], carry[:, 0:E], float(CAP), -1.0, ALU.min, ALU.mult))
            dve.tensor_tensor(starts[:], window0[:], firsts[:], ALU.add).then_inc(s["starts_done"], 1)
            dve.wait_ge(s["top_kept"], 2 * B)
            link(dve.tensor_tensor(pdiff[:], tv[:, 1, :], tv[:, 0, :], ALU.subtract))

            def weights_low(of, x, j):
                dve.wait_ge(s["w_high"], of(4, 2 * x + 1 + j))
                need(dve, s["y_ps"], of(2 * NCH, NCH * (x - 1)))
                dve.tensor_tensor((w1l, w2l)[j][x % 2][:], (w1, w2)[j][:], (w1h, w2h)[j][x % 2][:], ALU.subtract
                                  ).then_inc(s["w_low"], 1)

            for j in range(2):
                weights_low(lambda k, plus: plus, 0, j)

            def squares(of, u):
                if there(of, u):
                    dve.wait_ge(s["bT_high"], of(2 * NCH, u + 1))
                    need(dve, s["h_ps"], of(4 * NCH, 2 * u - 2))
                    dve.tensor_tensor(bTl[u % 2][:], bank[u % 2][:, 0:CH], bTh[u % 2][:], ALU.subtract
                                      ).then_inc(s["bT_low"], 1)
                if there(of, u - 4):
                    v = u - 4
                    dve.wait_ge(s["back_ps"], of(2 * NCH, v + 1))
                    need(dve, put[v % NCH], of(64, 32 * (v // NCH)))
                    dve.tensor_copy(ys[v % NCH], bank[7][:, 0:CH].rearrange("p (t d) -> p t d", t=2)
                             ).then_inc(s["y_out"], 1)
                if there(of, u - 1):
                    v = u - 1
                    dve.wait_ge(s["hr_done"], of(4 * NCH, 2 * v + 2))
                    need(dve, s["hl_done"], of(2 * NCH, v - 1))
                    dve.tensor_tensor(sq[v % 2][:, :SQ], hr[v % 2][:, :SQ], hr[v % 2][:, :SQ], ALU.mult).then_inc(s["sq_done"], 1)
                    dve.wait_ge(s["sq_done"], of(2 * NCH, v + 1))
                    dve.wait_ge(s["sq2_done"], of(2 * NCH, v + 1))
                    dve.wait_ge(s["hh_done"], of(2 * NCH, v + 1))
                    need(dve, s["y_ps"], of(2 * NCH, v - 1))
                    dve.tensor_tensor(hl[v % 2][:], sq[v % 2], hh[v % 2][:], ALU.subtract).then_inc(s["hl_done"], 1)
                if 2 <= u % NCH <= 3 and there(of, u):
                    weights_low(of, u // NCH + 1, u % NCH - 2)

            chunks(dve, squares, 4)

            link(dve.tensor_tensor(oh[:], ti[:, 1, :].unsqueeze(2).to_broadcast([P, B, E]),
                                   ioE[:].unsqueeze(1).to_broadcast([P, B, E]), ALU.is_equal))
            link(dve.tensor_tensor(oh[:], oh[:], carry[:, 0:E].unsqueeze(1).to_broadcast([P, B, E]), ALU.mult))
            link(dve.tensor_reduce(rank[:], oh[:], AX.X, ALU.add))
            dve.wait_ge(s["skipg"], 4 * NG)
            link(dve.tensor_tensor(ranks[:, 1, :], ranks[:, 1, :], rank[:], ALU.add))
            link(dve.tensor_scalar(valid[:], ranks[:], float(CAP), None, ALU.is_lt))
            dve.wait_ge(s["pe_done"], 1)
            link(dve.tensor_scalar(psumr[:], pe2[:], 1.0, None, ALU.add))
            link(dve.reciprocal(pdiff[:], psumr[:]))
            link(dve.tensor_tensor(pe2[:], pe2[:], pdiff[:], ALU.mult))
            dve.tensor_tensor(prob[:, 0, :], pdiff[:], valid[:, 0, :], ALU.mult).then_inc(s["prob_done"], 1)
            dve.tensor_tensor(prob[:, 1, :], pe2[:], valid[:, 1, :], ALU.mult).then_inc(s["prob_done"], 1)
            dve.wait_ge(s["prob_done"], 2)
            dve.wait_ge(s["x1_kept"], B)

            for g in range(NG):
                y = ya[g % YR]
                dve.wait_ge(ya_in[g % YR], 32 * (g // YR + 1))
                for t in range(G):
                    b = G * g + t
                    dve.scalar_tensor_tensor(out=xr[:, b, :], in0=y[1][:, t, :], scalar=prob[:, 1, b:b + 1],
                                             in1=xr[:, b, :], op0=ALU.mult, op1=ALU.add).then_inc(s["added"], 1)
                dve.wait_ge(s["added"], G * (g + 1))
                dve.wait_ge(s["weighted"], G * (g + 1))
                dve.tensor_tensor(xr[:, G * g:G * (g + 1), :], xr[:, G * g:G * (g + 1), :], y[0], ALU.add
                                  ).then_inc(s["summed"], 1)

        @block.tensor
        def _(pe):
            def turn_ctx(g):
                pe.wait_ge(s["c_inn"], g.times(16, 16))
                need(pe, s["qr_done"], g.times(1))
                if not g.known or g.base > 2:
                    pe.wait_ge(s["carried"], g.times(1, -3))
                for t in range(G):
                    mm = pe.transpose(bank[6][:, t * S:(t + 1) * S], c_in[:, t, :], ident[:])
                mm.then_inc(s["cT_ps"], 1)

            def project(w, turned, half, done):
                cols = slice(half * G * S // 2, (half + 1) * G * S // 2)
                mm = pe.matmul(bank[6][:, cols], w[:], turned[:, cols], start=True, stop=True)
                if half:
                    mm.then_inc(s[done], 1)

            def project_k(g, halves=(0, 1)):
                if 0 in halves:
                    pe.wait_ge(s["cT_out"], g.times(1, 1))
                for half in halves:
                    project(wk_s, cTA, half, "k_ps")

            def project_v(g):
                if g.known and g.base == 0:
                    pe.wait_ge(s["v_in"], 32)
                pe.wait_ge(s["kr_done"], g.times(1, 1))
                for t in range(G):
                    mm = pe.matmul(bank[6][:, t * D:(t + 1) * D], cTA[:, t * S:(t + 1) * S], wv_s[:],
                                   start=True, stop=True)
                mm.then_inc(s["v_ps"], 1)

            def turn_x(g):
                pe.wait_ge(s["xnA_done"], g.times(4, G))
                pe.wait_ge(s["v_out"], g.times(1, 1))
                for t in range(G):
                    mm = pe.transpose(bank[6][:, t * S:(t + 1) * S], xnA[:, t, :], ident[:])
                mm.then_inc(s["xT_ps"], 1)

            def project_q(g, halves=(0, 1)):
                if 0 in halves:
                    pe.wait_ge(s["xT_out"], g.times(1, 1))
                for half in halves:
                    project(wq_s, xTA, half, "q_ps")

            first, second = At(0, mult=1), At(1, mult=1)
            pe.wait_ge(s["rt"], 3)
            turn_ctx(first)
            pe.wait_ge(s["wperm"], 1)
            project_k(first)
            pe.wait_ge(s["g_in"], 16)
            pe.transpose(bank[7][:, 0:E], wg_raw[:], ident[0:E, 0:E]).then_inc(s["wgT_ps"], 1)
            project_v(first)
            turn_x(first)
            pe.wait_ge(s["wperm"], 2)
            project_q(first)
            for part in (turn_ctx, project_k, project_v, turn_x, project_q):
                part(second)
            pe.wait_ge(s["wgT_out"], 1)

            def scores_for_max(b, c):
                i = b.base % 4
                if c == 0:
                    pe.wait_ge(q_in[i], b.rounds16())
                    pe.wait_ge(km_in[i], b.rounds16())
                need(pe, s["mx"], b.times(4, c - 1))
                for h in range(HC):
                    cols = slice((HC * c + h) * S, (HC * c + h + 1) * S)
                    mm = pe.matmul(bank[c % 2][:, h * S:(h + 1) * S], qs[i][:, cols], km[i][:, cols],
                                   start=True, stop=True)
                mm.then_inc(s["s1"], 1)

            def scores_for_exp(b, c):
                i = b.base % 4
                if c == 0:
                    pe.wait_ge(k_in[i], b.rounds16(16))
                    pe.wait_ge(m_in[i], b.rounds16())
                need(pe, s["ex"], b.times(4, c - 1))
                for h in range(HC):
                    cols = slice((HC * c + h) * S, (HC * c + h + 1) * S)
                    mm = pe.matmul(bank[2 + c % 2][:, h * S:(h + 1) * S], ks[i][:, cols], qs[i][:, cols],
                                   start=True, stop=True)
                mm.then_inc(s["s2"], 1)

            def times_v(b, c):
                pe.wait_ge(s["ex"], b.times(4, c + 1))
                if c == 0:
                    pe.wait_ge(s["va_in"], b.times(1, 1))
                    need(pe, s["av_out"], b.times(1))
                for h in range(HC):
                    mm = pe.matmul(bank[4][VW * h:VW * (h + 1), c * S:(c + 1) * S],
                                   va[b.base % 2][:, HC * c + h, :], pr[c][:, h * S:(h + 1) * S],
                                   start=True, stop=True, tile_position=(0, VW * h))
                mm.then_inc(s["av"], 1)

            def context_back(b):
                pe.wait_ge(s["av_out"], b.times(1, 1))
                need(pe, s["x1_done"], b.times(1))
                for c in range(NC):
                    mm = pe.transpose(bank[5][:, c * S:(c + 1) * S], avs[:, c * S:(c + 1) * S], ident[:])
                mm.then_inc(s["nat"], 1)

            def context_turned(b):
                pe.wait_ge(s["cn_done"], b.times(1, 1))
                pe.transpose(bank[5][:, 0:128], cn[:], ident[:]).then_inc(s["cnT_ps"], 1)

            def output_rows(b):
                if b.known and b.base == 0:
                    pe.wait_ge(s["o_in"], 32)
                pe.wait_ge(s["cnT_out"], b.times(1, 1))
                pe.matmul(bank[5][:, 128:256], cnT[:], wo_s[:], start=True, stop=True).then_inc(s["wo_ps"], 1)

            def maxima_turned(b):
                pe.wait_ge(s["n3"], b.times(1, 1))
                if b.known and b.base < 4:
                    need(pe, s["nT_out"], b.base)
                need(pe, s["xsT_out"], b.times(1, -3))
                pe.transpose(bank[7][:, 0:S // 2].bitcast(BF16), nparts_pad[:], identb[:]).then_inc(s["nT_ps"], 1)

            def normed_turned(b):
                pe.wait_ge(s["xs_done"], b.times(1, 1))
                pe.wait_ge(s["nT_out"], min(b.base + 4, B) if b.known else b.times(1, 4))
                need(pe, s["idx_done"], b.times(1))
                pe.transpose(bank[7][:, 128:256], xs[b.base % 2][:], ident[:]).then_inc(s["xsT_ps"], 1)

            def logits(b):
                pe.wait_ge(s["xsT_out"], b.times(1, 1))
                pe.wait_ge(s["nT_out"], min(b.base + 5, B) if b.known else b.times(1, 5))
                pe.matmul(bank[7][:, 256:256 + E], xsT[:], wgT[:], start=True, stop=True).then_inc(s["lg"], 1)

            def count_group(q):
                pe.wait_ge(s["ohg_done"], q.times(2, 2))
                pe.wait_ge(s["qr_done"], min(q.base + 4, NG) if q.known else q.times(1, 4))
                need(pe, s["carried"], q.times(1))
                n = TOP_K * E
                pe.matmul(bank[6][:, 0:G * n], before[:], ohg[:].rearrange("p t e -> p (t e)"),
                          start=True, stop=False, skip_group_check=True)
                for t in range(G):
                    mm = pe.matmul(bank[6][:, (t + 1) * n:(G + 1) * n].rearrange("p (g e) -> p g e", e=n), onesb[:],
                                   ohg[:, t:t + 1, :].to_broadcast([P, G - t, n]),
                                   start=False, stop=(t == G - 1), skip_group_check=True)
                mm.then_inc(s["rkg_ps"], 1)

            def step(j, u, r):
                g, q = group_of(r), ranked(r)
                ahead, now, last, second, third = j + 2, j, j + (-1), j + (-2), j + (-3)
                if live(ahead):
                    scores_for_max(ahead, 0)
                if live(second):
                    output_rows(second)
                if live(ahead):
                    scores_for_max(ahead, 1)
                if live(now):
                    scores_for_exp(now, 0)
                if u == 0 and g is not None:
                    turn_ctx(g)
                if live(now):
                    scores_for_exp(now, 1)
                if u == 1 and g is not None:
                    project_k(g, (1,))
                if live(j + 1):
                    maxima_turned(j + 1)
                if live(last):
                    context_back(last)
                if u == 2 and g is not None:
                    turn_x(g)
                if live(now):
                    times_v(now, 0)
                if live(ahead):
                    scores_for_max(ahead, 2)
                if live(third):
                    logits(third)
                if live(now):
                    scores_for_exp(now, 2)
                if u == 2 and g is not None:
                    project_q(g, (0,))
                if live(now):
                    times_v(now, 1)
                if live(last):
                    context_turned(last)
                if live(now):
                    scores_for_exp(now, 3)
                if live(ahead):
                    scores_for_max(ahead, 3)
                if live(now):
                    times_v(now, 2)
                if u == 3 and q is not None:
                    count_group(q)
                if live(second):
                    normed_turned(second)
                if u == 0 and g is not None:
                    project_k(g, (0,))
                if u == 2 and g is not None:
                    project_q(g, (1,))
                if u == 1 and g is not None:
                    project_v(g)
                if live(now):
                    times_v(now, 3)

            steps(pe, step, (2,))

            def three_passes(out_, wh, wl, bh, bl, first, last_):
                pe.matmul(out_, wh, bh, start=first, stop=False)
                pe.matmul(out_, wl, bh, start=False, stop=False)
                return pe.matmul(out_, wh, bl, start=False, stop=last_)

            def experts(of, u):
                if there(of, u):
                    pe.wait_ge(br_in[u], of(16, 16))
                    need(pe, s["bT_low"], of(2 * NCH, u - 1))
                    for t in range(2):
                        mm = pe.transpose(bank[u % 2][:, t * P:(t + 1) * P], br[u][:, t, 0:D], ident[:])
                    mm.then_inc(s["bT_ps"], 1)
                if there(of, u - 1):
                    v = u - 1
                    i, w = v % 2, v // NCH % 2
                    if v % NCH == 0:
                        pe.wait_ge(s["w_low"], of(4, 2 * (v // NCH) + 2))
                    pe.wait_ge(s["bT_low"], of(2 * NCH, v + 1))
                    need(pe, s["hr_done"], of(4 * NCH, 2 * v - 2))
                    for f in range(NF):
                        cols = slice(f * P, (f + 1) * P)
                        mm = three_passes(bank[2 + 2 * i + f // 2][:, (f % 2) * CH:(f % 2 + 1) * CH],
                                          w1h[w][:, cols], w1l[w][:, cols], bTh[i][:], bTl[i][:], True, True)
                        if f % 2:
                            mm.then_inc(s["h_ps"], 1)
                if there(of, u - 3):
                    v = u - 3
                    i, w = v % 2, v // NCH % 2
                    pe.wait_ge(s["hl_done"], of(2 * NCH, v + 1))
                    need(pe, s["yT_out"], of(2 * NCH, v))
                    for f in range(NF):
                        cols, part = slice(f * D, (f + 1) * D), slice(f * CH, (f + 1) * CH)
                        mm = three_passes(bank[6][:, 0:CH], w2h[w][:, cols], w2l[w][:, cols],
                                          hh[i][:, part], hl[i][:, part], f == 0, f == NF - 1)
                    mm.then_inc(s["y_ps"], 1)
                if there(of, u - 4):
                    v = u - 4
                    pe.wait_ge(s["yT_out"], of(2 * NCH, v + 1))
                    need(pe, s["y_out"], of(2 * NCH, v))
                    for t in range(2):
                        mm = pe.transpose(bank[7][:, t * P:(t + 1) * P], yT[v % 2][:, t * P:(t + 1) * P], ident[:])
                    mm.then_inc(s["back_ps"], 1)

            chunks(pe, experts, 4)


_INS = ['x', 'ctx_1024', 'L0_xattn_Wq', 'L0_xattn_bq', 'L0_xattn_Wk', 'L0_xattn_bk', 'L0_xattn_Wv', 'L0_xattn_bv',
        'L0_xattn_Wo', 'L0_xattn_bo', 'L0_ffn_w_g', 'L0_ffn_c_fc', 'L0_ffn_c_proj']
_OUT = ((32, 128, 128), 'float32')


def kernel(**inputs):
    import numpy as np
    import concourse.bacc as bacc
    from concourse.bass_utils import run_bass_kernel_spmd as run

    nc = bacc.Bacc("TRN2", target_bir_lowering=False, num_devices=1)
    arrays, args = {}, []
    for name in _INS:
        a = np.ascontiguousarray(inputs[name])
        arrays[f"in_{name}"] = a
        args.append(nc.dram_tensor(f"in_{name}", a.shape, mybir.dt.from_np(a.dtype), kind="ExternalInput").ap())
    shape, dtype = _OUT
    args.append(nc.dram_tensor("out_0", shape, mybir.dt.from_np(np.dtype(dtype)), kind="ExternalOutput").ap())
    xattn_moe_kernel(nc, *args)
    r = run(nc, [arrays], core_ids=[0])
    return r.results[0]["out_0"]
```
